# Optimizing a Trainium2 kernel written in Bass

```python
import numpy as np
import jax
import jax.numpy as jnp

def _softmax(x, axis=-1):
    return jax.nn.softmax(x, axis=axis)

def _gelu(x):
    return jax.nn.gelu(x, approximate=True)

def _silu(x):
    return jax.nn.silu(x)

def _sigmoid(x):
    return jax.nn.sigmoid(x)

def _layernorm(x, axis=-1, eps=1e-05):
    m = jnp.mean(x, axis=axis, keepdims=True)
    v = jnp.var(x, axis=axis, keepdims=True)
    return (x - m) / jnp.sqrt(v + eps)

def _scatter_add(tgt, idx, src, axis=0):
    return tgt.at[idx].add(src)

def _segment_sum(src, seg, n):
    return jax.ops.segment_sum(src, seg, n)
kernel_name = 'mk_gnn_resnorm_d1_gnn_r64_e00aa3'

def setup_inputs(seed: int=0):
    np.random.seed(seed)
    _w = jnp.asarray

    def _rec_inputs():
        import jax
        import jax.numpy as jnp
        _gk = jax.random.key(seed)
        x = -6.415e-05 + 1 * jax.random.normal(jax.random.fold_in(_gk, 1), (20000, 512), jnp.float32)
        src = jax.random.randint(jax.random.fold_in(_gk, 2), (5000,), 0, 20000, jnp.int32)
        dst = jax.random.randint(jax.random.fold_in(_gk, 3), (5000,), 0, 20000, jnp.int32)
        _o = jnp.argsort(dst, stable=True)
        src = src[_o]
        dst = dst[_o]
        return (x, src, dst)
    x, src, dst = _rec_inputs()

    def _L0_gnn_setup():
        import jax, jax.numpy as jnp
        import numpy as np
        N_NODES = 20000
        N_EDGES = 5000
        D_IN = 512
        D_HID = 512
        EPS = 1e-05

        def _xavier(key, shape):
            fan_in, fan_out = (shape[1], shape[0])
            limit = np.sqrt(6.0 / (fan_in + fan_out)).astype(np.float32)
            return jax.random.uniform(key, shape, jnp.float32, -limit, limit)

        def _sage_conv(h, src, dst, Wl, bl, Wr):
            msg = h[src]
            s = jax.ops.segment_sum(msg, dst, num_segments=N_NODES)
            cnt = jax.ops.segment_sum(jnp.ones((src.shape[0], 1), h.dtype), dst, num_segments=N_NODES)
            agg = s / jnp.maximum(cnt, 1.0)
            return agg @ Wl.T + bl + h @ Wr.T

        def _layer_norm(h, g, b):
            mu = jnp.mean(h, axis=-1, keepdims=True)
            var = jnp.mean((h - mu) ** 2, axis=-1, keepdims=True)
            return (h - mu) * jax.lax.rsqrt(var + EPS) * g + b

        def _prelu(h, a):
            return jnp.where(h >= 0, h, a * h)
        key = jax.random.key(seed)
        ks = jax.random.split(key, 16)
        x = jax.random.normal(ks[0], (N_NODES, D_IN), jnp.float32)
        edge_index = jax.random.randint(ks[1], (2, N_EDGES), 0, N_NODES, jnp.int64)
        dims = [(D_IN, D_HID), (D_HID, D_HID), (D_HID, D_HID)]
        inp = {'x': x, 'edge_index': edge_index}
        for i, (din, dout) in enumerate(dims):
            inp[f'Wl{i}'] = _xavier(ks[2 + 3 * i], (dout, din))
            inp[f'bl{i}'] = jnp.zeros((dout,), jnp.float32)
            inp[f'Wr{i}'] = _xavier(ks[3 + 3 * i], (dout, din))
            inp[f'g{i}'] = jnp.ones((dout,), jnp.float32)
            inp[f'b{i}'] = jnp.zeros((dout,), jnp.float32)
        inp['a_prelu'] = jnp.full((1,), 0.25, jnp.float32)
        return inp
    _L0_gnn_all = _L0_gnn_setup()
    _L0_gnn_in = {k: v for k, v in _L0_gnn_all.items() if k in ('Wl0', 'bl0', 'Wr0', 'g0', 'b0', 'Wl1', 'bl1', 'Wr1', 'g1', 'b1', 'Wl2', 'bl2', 'Wr2', 'g2', 'b2', 'a_prelu')}
    del _L0_gnn_all
    return {'x': x, 'src': src, 'dst': dst, 'L0_gnn_Wl0': _L0_gnn_in['Wl0'], 'L0_gnn_bl0': _L0_gnn_in['bl0'], 'L0_gnn_Wr0': _L0_gnn_in['Wr0'], 'L0_gnn_g0': _L0_gnn_in['g0'], 'L0_gnn_b0': _L0_gnn_in['b0'], 'L0_gnn_Wl1': _L0_gnn_in['Wl1'], 'L0_gnn_bl1': _L0_gnn_in['bl1'], 'L0_gnn_Wr1': _L0_gnn_in['Wr1'], 'L0_gnn_g1': _L0_gnn_in['g1'], 'L0_gnn_b1': _L0_gnn_in['b1'], 'L0_gnn_Wl2': _L0_gnn_in['Wl2'], 'L0_gnn_bl2': _L0_gnn_in['bl2'], 'L0_gnn_Wr2': _L0_gnn_in['Wr2'], 'L0_gnn_g2': _L0_gnn_in['g2'], 'L0_gnn_b2': _L0_gnn_in['b2'], 'L0_gnn_a_prelu': _L0_gnn_in['a_prelu']}

def reference(x, src, dst, L0_gnn_Wl0, L0_gnn_bl0, L0_gnn_Wr0, L0_gnn_g0, L0_gnn_b0, L0_gnn_Wl1, L0_gnn_bl1, L0_gnn_Wr1, L0_gnn_g1, L0_gnn_b1, L0_gnn_Wl2, L0_gnn_bl2, L0_gnn_Wr2, L0_gnn_g2, L0_gnn_b2, L0_gnn_a_prelu):
    import jax
    import jax.numpy as jnp

    def _L0_gnn_ref(x, edge_index, Wl0, bl0, Wr0, g0, b0, Wl1, bl1, Wr1, g1, b1, Wl2, bl2, Wr2, g2, b2, a_prelu):
        import jax, jax.numpy as jnp
        import numpy as np
        N_NODES = 20000
        N_EDGES = 5000
        D_IN = 512
        D_HID = 512
        EPS = 1e-05

        def _xavier(key, shape):
            fan_in, fan_out = (shape[1], shape[0])
            limit = np.sqrt(6.0 / (fan_in + fan_out)).astype(np.float32)
            return jax.random.uniform(key, shape, jnp.float32, -limit, limit)

        def _sage_conv(h, src, dst, Wl, bl, Wr):
            msg = h[src]
            s = jax.ops.segment_sum(msg, dst, num_segments=N_NODES)
            cnt = jax.ops.segment_sum(jnp.ones((src.shape[0], 1), h.dtype), dst, num_segments=N_NODES)
            agg = s / jnp.maximum(cnt, 1.0)
            return agg @ Wl.T + bl + h @ Wr.T

        def _layer_norm(h, g, b):
            mu = jnp.mean(h, axis=-1, keepdims=True)
            var = jnp.mean((h - mu) ** 2, axis=-1, keepdims=True)
            return (h - mu) * jax.lax.rsqrt(var + EPS) * g + b

        def _prelu(h, a):
            return jnp.where(h >= 0, h, a * h)
        src, dst = (edge_index[0], edge_index[1])
        params = [(Wl0, bl0, Wr0, g0, b0), (Wl1, bl1, Wr1, g1, b1), (Wl2, bl2, Wr2, g2, b2)]
        h = x
        residual = 0.0
        for Wl, bl, Wr, g, b in params:
            h = residual + _sage_conv(h, src, dst, Wl, bl, Wr)
            h = _layer_norm(h, g, b)
            h = _prelu(h, a_prelu)
            residual = h
        return h
    edge_index = jnp.stack([src, dst])
    x = _layernorm(x + _L0_gnn_ref(x, edge_index, L0_gnn_Wl0, L0_gnn_bl0, L0_gnn_Wr0, L0_gnn_g0, L0_gnn_b0, L0_gnn_Wl1, L0_gnn_bl1, L0_gnn_Wr1, L0_gnn_g1, L0_gnn_b1, L0_gnn_Wl2, L0_gnn_bl2, L0_gnn_Wr2, L0_gnn_g2, L0_gnn_b2, L0_gnn_a_prelu), axis=-1)
    return x

_drawn_inputs = setup_inputs


def setup_inputs(seed=0):
    import zlib

    import numpy as np

    out = dict(_drawn_inputs(seed))
    spreads = {'L0_gnn_bl0': (0.0, 0.1),
     'L0_gnn_g0': (1.0, 0.2),
     'L0_gnn_b0': (0.0, 0.1),
     'L0_gnn_bl1': (0.0, 0.1),
     'L0_gnn_g1': (1.0, 0.2),
     'L0_gnn_b1': (0.0, 0.1),
     'L0_gnn_bl2': (0.0, 0.1),
     'L0_gnn_g2': (1.0, 0.2),
     'L0_gnn_b2': (0.0, 0.1)}
    factors = {}
    for name, (base, spread) in spreads.items():
        noise = np.random.default_rng([zlib.crc32(name.encode()), seed]).standard_normal(out[name].shape)
        drawn = base * np.exp(spread * noise) if base else spread * noise
        out[name] = jnp.asarray(drawn.astype(out[name].dtype))
    for name, factor in factors.items():
        out[name] = (out[name] * factor).astype(out[name].dtype)
    return out
```

```python
from contextlib import ExitStack

import numpy as np

import concourse.bass as bass
from concourse import mybir

P = 128
ALU = mybir.AluOpType
ACT = mybir.ActivationFunctionType
F32 = mybir.dt.float32
F32R = mybir.dt.float32r
I32 = mybir.dt.int32
I16 = mybir.dt.int16

L = 3
TG = 4
UG = L * TG
EPS = 1e-5
FAR = 65536.0


def reach(eng, sem, count):
    if isinstance(count, int) and count <= 0:
        return
    eng.wait_ge(sem, count)


def build_program(nc, x, src, dst, Wl, bl, Wr, g, b, a_prelu, ident_in, edge_no_in, row_select_in,
                  dst_pad_in, src_pad_in, out):
    N, D = x.shape
    E = src.shape[0]
    KC = D // P
    GROUP = TG * P
    NG = N // GROUP
    REST = N - NG * GROUP
    ET = -(-E // P)
    EP = ET * P
    AB = 4
    assert N < 2 ** 15 and D == 512 and NG % 2 == 1 and NG >= 5 and 0 < REST <= P and ET % AB == 0 and ET >= 2 * AB
    NU = UG * NG
    UNITS = NU + L

    h_dram = [nc.dram_tensor(f"h{l + 1}_scratch", [N, D], F32).ap() for l in range(L - 1)]
    dst_dram = nc.dram_tensor("dst_padded", [EP + 2], I32).ap()
    src_dram = nc.dram_tensor("src_padded", [EP], I32).ap()

    with ExitStack() as ctx:
        def sb(name, shape, dt=F32):
            return ctx.enter_context(nc.sbuf_tensor(name, shape, dt))

        def sem(name):
            return ctx.enter_context(nc.semaphore(name))

        w_hi = [sb(f"w_hi{i}", [P, KC, D], F32R) for i in range(2 * L)]
        w_lo = [sb(f"w_lo{i}", [P, KC, D], F32R) for i in range(2 * L)]
        bias2 = sb("bias2", [2, L, D], F32R)
        ones2 = sb("ones2", [2, P], F32R)
        gain = sb("gain", [P, L, D])
        shift = sb("shift", [P, L, D])
        slope = sb("slope", [P, 1])
        minus_slope = sb("minus_slope", [P, 1])
        minus_half = sb("minus_half", [P, 1])
        ident = sb("ident", [P, P])

        x_sb = [sb(f"x_sb{i}", [P, TG, D]) for i in range(2)]
        h_sb = [sb(f"h_sb{i}", [P, TG, D]) for i in range(L - 1)]
        o_sb = [sb(f"o_sb{i}", [P, TG, D]) for i in range(2)]
        hT_hi = [sb(f"hT_hi{i}", [P, KC, P], F32R) for i in range(2)]
        hT_lo = [sb(f"hT_lo{i}", [P, KC, P], F32R) for i in range(2)]
        y = [sb(f"y{i}", [P, D]) for i in range(2)]
        pos = [sb(f"pos{i}", [P, D]) for i in range(2)]
        stats = [sb(f"stats{i}", [P, 6]) for i in range(2)]
        mv = [sb(f"mv{i}", [P, 2]) for i in range(2)]
        veps = [sb(f"veps{i}", [P, 1]) for i in range(2)]
        rstd = [sb(f"rstd{i}", [P, 1]) for i in range(2)]
        ostats = sb("ostats", [P, 6])
        omv = [sb(f"omv{i}", [P, 2]) for i in range(2)]
        oveps = [sb(f"oveps{i}", [P, 1]) for i in range(2)]
        orstd = [sb(f"orstd{i}", [P, 1]) for i in range(2)]

        dst_row = sb("dst_row", [P, EP + 1], I16)
        rows_of = sb("rows_of", [P, ET, 3], I32)
        rcount = sb("rcount", [P, ET])
        dst_col = sb("dst_col", [P, ET])
        gather_rows = [sb(f"gather_rows{i}", [P, 2], I32) for i in range(AB)]
        x_rows = [sb(f"x_rows{i}", [P, 1], I32) for i in range(AB)]
        scatter_rows = [sb(f"scatter_rows{i}", [P, 1], I32) for i in range(AB)]
        same = [sb(f"same{i}", [P, P], F32R) for i in range(2)]
        m_hi = [sb(f"m_hi{i}", [P, D], F32R) for i in range(2)]
        m_lo = [sb(f"m_lo{i}", [P, D], F32R) for i in range(2)]
        sT_hi = [sb(f"sT_hi{i}", [P, KC, P], F32R) for i in range(2)]
        sT_lo = [sb(f"sT_lo{i}", [P, KC, P], F32R) for i in range(2)]

        ps = [ctx.enter_context(nc.psum_tensor(f"ps{i}", [P, D], F32)) for i in range(8)]
        ps_t, ps_z, ps_a, ps_s = ps[0:2], ps[2:4], ps[4:6], ps[6:8]

        passed = {e: sem(f"passed_{e}") for e in ("dve", "pool")}

        stage = [o_sb[0], o_sb[1], h_sb[0], h_sb[1]]
        WORDER = [("r", l) for l in range(L)] + [("l", l) for l in range(L)]

        with ExitStack() as sctx:
            def ssb(name, shape, dt=F32):
                return sctx.enter_context(nc.sbuf_tensor(name, shape, dt))

            def ssem(name):
                return sctx.enter_context(nc.semaphore(name))

            room, room2 = [t[:].rearrange("p j d -> p (j d)") for t in x_sb]
            lists = room[0:ET, 0:4 * P].bitcast(I32).rearrange("t (c p) -> t c p", c=4)
            listf = room[0:ET, 4 * P:8 * P].rearrange("t (c p) -> t c p", c=4)
            cols = room[0:ET, 8 * P:13 * P].rearrange("t (c p) -> t c p", c=5)
            edge_no = room[0:ET, 13 * P:14 * P]
            first = room[0:ET, 14 * P:15 * P]
            run = room[0:ET, 15 * P:16 * P]
            bias_raw = room2[0:2, 0:L * D]
            last_run = room2[0:ET, L * D:L * D + 1]
            before = room2[0:ET, L * D + 1:L * D + 2]
            row_select = room2[0:2, L * D + 2:L * D + 4]
            runs_before = room2[0:1, L * D + 4:L * D + 5 + ET]
            zero_row = room2[0:1, L * D + 64:L * D + 64 + ET]
            bias_flat = bias2[:].rearrange("p l d -> p (l d)")

            w_in = [ssem(f"w_in{i}") for i in range(4)]
            ident_in_sem = ssem("ident_in_sem")
            const_in = ssem("const_in")
            lists_copied = ssem("lists_copied")
            lists_in = ssem("lists_in")
            row_in = ssem("row_in")
            w_turned = ssem("w_turned")
            w_diag = ssem("w_diag")
            w_high = ssem("w_high")
            w_low = ssem("w_low")
            prep = ssem("prep")
            sentinel = ssem("sentinel")
            small_turned = ssem("small_turned")
            run_done = ssem("run_done")

            CONSTS = 3 + 3 * L
            with nc.Block() as block:
                @block.sync
                def _(sp):
                    def load_weight(i):
                        side, l = WORDER[i]
                        w = (Wr if side == "r" else Wl)[l]
                        if i >= 4:
                            sp.wait_ge(w_turned, KC * (i - 3))
                        sp.dma_start(stage[i % 4][:], w.rearrange("(c p) k -> p c k", p=P)).then_inc(w_in[i % 4], 16)

                    sp.dma_start(ident[:], ident_in).then_inc(ident_in_sem, 16)
                    load_weight(0)
                    sp.dma_start(dst_dram[1:E + 1], dst).then_inc(lists_copied, 16)
                    sp.dma_start(dst_dram[0:1], dst_pad_in[0:1]).then_inc(lists_copied, 16)
                    sp.dma_start(dst_dram[E + 1:EP + 2], dst_pad_in[1:EP - E + 2]).then_inc(lists_copied, 16)
                    sp.dma_start(src_dram[0:E], src).then_inc(lists_copied, 16)
                    if EP > E:
                        sp.dma_start(src_dram[E:EP], src_pad_in[0:EP - E]).then_inc(lists_copied, 16)
                    load_weight(1)
                    load_weight(2)
                    sp.dma_start(edge_no, edge_no_in).then_inc(const_in, 16)
                    sp.dma_start(row_select, row_select_in).then_inc(const_in, 16)
                    sp.dma_start(slope[:], a_prelu.rearrange("(a c) -> a c", a=1).to_broadcast([P, 1])).then_inc(const_in, 16)
                    for l in range(L):
                        sp.dma_start(bias_raw[:, l * D:(l + 1) * D], bl[l].rearrange("(a d) -> a d", a=1).to_broadcast([2, D])).then_inc(const_in, 16)
                        sp.dma_start(gain[:, l, :], g[l].rearrange("(a d) -> a d", a=1).to_broadcast([P, D])).then_inc(const_in, 16)
                        sp.dma_start(shift[:, l, :], b[l].rearrange("(a d) -> a d", a=1).to_broadcast([P, D])).then_inc(const_in, 16)
                    sp.wait_ge(lists_copied, 16 * (4 + (EP > E)))
                    tiled = lambda v: v.rearrange("(t p) -> t p", p=P)
                    sp.dma_start(lists[:, 0, :], tiled(dst_dram[1:EP + 1])).then_inc(lists_in, 16)
                    sp.dma_start(lists[:, 1, :], tiled(dst_dram[2:EP + 2])).then_inc(lists_in, 16)
                    sp.dma_start(lists[:, 2, :], tiled(dst_dram[0:EP])).then_inc(lists_in, 16)
                    sp.dma_start(lists[:, 3, :], tiled(src_dram)).then_inc(lists_in, 16)
                    for i in range(3, 2 * L):
                        load_weight(i)

                @block.tensor
                def _(pe):
                    pe.wait_ge(ident_in_sem, 16)
                    for i in range(2 * L):
                        pe.wait_ge(w_in[i % 4], 16 * (i // 4 + 1))
                        for k in range(KC):
                            n = KC * i + k
                            if n >= 2:
                                pe.wait_ge(w_low, n - 1)
                            for c in range(KC):
                                mm = pe.transpose(ps_t[n % 2][:, c * P:(c + 1) * P],
                                                  stage[i % 4][:, c, k * P:(k + 1) * P], ident[:])
                            mm.then_inc(w_turned, 1)
                    pe.wait_ge(prep, 8)
                    pe.transpose(ps_z[0][0:1, 0:ET], last_run, ident[0:ET, 0:ET]).then_inc(small_turned, 1)
                    pe.wait_ge(prep, 9)
                    pe.transpose(ps_z[1][0:ET, 0:1], runs_before[0:1, 0:ET], ident[0:1, 0:1]).then_inc(small_turned, 1)
                    pe.wait_ge(prep, 16)
                    for c in range(5):
                        mm = pe.transpose(ps_a[0][:, c * ET:(c + 1) * ET], cols[:, c, :], ident[0:ET, 0:ET])
                    mm.then_inc(small_turned, 1)

                @block.scalar
                def _(act):
                    for i in range(2 * L):
                        side, l = WORDER[i]
                        for k in range(KC):
                            n = KC * i + k
                            if side == "r" and l > 0:
                                act.wait_ge(w_diag, KC * (i - 1) + k + 1)
                            else:
                                act.wait_ge(w_turned, n + 1)
                            nc.scalar.copy(w_hi[i][:, k, :], ps_t[n % 2][:]).then_inc(w_high, 1)

                @block.gpsimd
                def _(pool):
                    pool.wait_ge(lists_copied, 16 * (4 + (EP > E)))
                    pool.dma_start(dst_row[:], dst_dram[0:EP + 1].rearrange("(a d) -> a d", a=1)
                                   .to_broadcast([P, EP + 1])).then_inc(row_in, 16)
                    pool.wait_ge(row_in, 16)

                @block.vector
                def _(dve):
                    dve.wait_ge(ident_in_sem, 16)
                    nc.vector.memset(ones2[:].bitcast(F32), 1.0)
                    nc.vector.memset(minus_half[:], -0.5)
                    nc.vector.memset(runs_before[:, 0:1], 0.0)
                    nc.vector.memset(zero_row, 0.0)
                    for i in range(2 * L):
                        side, l = WORDER[i]
                        for k in range(KC):
                            n = KC * i + k
                            if side == "r" and l > 0:
                                dve.wait_ge(w_turned, n + 1)
                                diag = ps_t[n % 2][:, k * P:(k + 1) * P]
                                nc.vector.tensor_tensor(diag, diag, ident[:], ALU.add).then_inc(w_diag, 1)
                            dve.wait_ge(w_high, n + 1)
                            nc.vector.tensor_tensor(w_lo[i][:, k, :], ps_t[n % 2][:],
                                                    w_hi[i][:, k, :].bitcast(F32), ALU.subtract).then_inc(w_low, 1)

                    step = [0]

                    def then(ins):
                        step[0] += 1
                        ins.then_inc(prep, 1)
                        dve.wait_ge(prep, step[0])

                    dve.wait_ge(const_in, 16 * CONSTS)
                    then(nc.vector.tensor_copy(bias_flat, bias_raw))
                    then(nc.vector.tensor_tensor(bias_raw, bias_raw, bias_flat.bitcast(F32), ALU.subtract))
                    then(nc.vector.tensor_scalar(bias_flat, bias_flat.bitcast(F32), row_select[:, 0:1], None, ALU.mult))
                    then(nc.vector.scalar_tensor_tensor(bias_flat, bias_raw, row_select[:, 1:2], bias_flat.bitcast(F32),
                                                        ALU.mult, ALU.add))
                    dve.wait_ge(lists_in, 64)
                    then(nc.vector.tensor_copy(listf, lists))
                    then(nc.vector.tensor_tensor(first, listf[:, 0, :], listf[:, 2, :], ALU.not_equal))
                    then(nc.vector.tensor_tensor(first, first, edge_no, ALU.mult))
                    nc.vector.tensor_tensor_scan(run, first, first, 0.0, ALU.max, ALU.max).then_inc(run_done, 1)
                    dve.wait_ge(run_done, 1)
                    then(nc.vector.tensor_copy(last_run, run[:, P - 1:P]))
                    dve.wait_ge(small_turned, 1)
                    then(nc.vector.tensor_tensor_scan(runs_before[:, 1:ET + 1], ps_z[0][0:1, 0:ET], zero_row,
                                                      0.0, ALU.max, ALU.max))
                    dve.wait_ge(small_turned, 2)
                    then(nc.vector.tensor_copy(before, ps_z[1][0:ET, 0:1]))
                    then(nc.vector.tensor_scalar(run, run, before[:, 0:1], -1.0, ALU.max, ALU.mult))
                    then(nc.vector.scalar_tensor_tensor(first, edge_no, 1.0, run, ALU.add, ALU.add))
                    then(nc.vector.reciprocal(cols[:, 3, :], first))
                    nc.vector.tensor_copy(cols[:, 0, :], listf[:, 3, :])
                    nc.vector.tensor_copy(cols[:, 4, :], listf[:, 0, :])
                    then(nc.vector.tensor_scalar(cols[:, 1, :], listf[:, 0, :], float(N - 1), None, ALU.min))
                    then(nc.vector.tensor_tensor(run, listf[:, 0, :], listf[:, 1, :], ALU.is_equal))
                    then(nc.vector.scalar_tensor_tensor(cols[:, 2, :], run, FAR, listf[:, 0, :], ALU.mult, ALU.add))
                    dve.wait_ge(small_turned, 3)
                    nc.vector.tensor_copy(rows_of[:].rearrange("p t c -> p c t"),
                                          ps_a[0][:, 0:3 * ET].rearrange("p (c t) -> p c t", c=3))
                    nc.vector.tensor_copy(rcount[:], ps_a[0][:, 3 * ET:4 * ET])
                    nc.vector.tensor_copy(dst_col[:], ps_a[0][:, 4 * ET:5 * ET])
                    nc.vector.tensor_scalar(minus_slope[:], slope[:], -1.0, None, ALU.mult)

        x_in = [sem(f"x_in{i}") for i in range(2)]
        turned = sem("turned")
        high = sem("high")
        low = sem("low")
        z_ready = sem("z_ready")
        stat_done = sem("stat_done")
        mv_done = sem("mv_done")
        gained = sem("gained")
        veps_done = sem("veps_done")
        rstd_done = sem("rstd_done")
        scaled = sem("scaled")
        shifted = sem("shifted")
        parted = sem("parted")
        h_done = sem("h_done")
        summed = sem("summed")
        ostat_done = sem("ostat_done")
        omv_done = sem("omv_done")
        oveps_done = sem("oveps_done")
        orstd_done = sem("orstd_done")
        o_done = sem("o_done")
        h_stored = [sem(f"h_stored{i}") for i in range(L - 1)]
        o_stored = [sem(f"o_stored{i}") for i in range(2)]

        class Unit:

            def __init__(self, half, par, k):
                while k < 0:
                    half, par, k = (half, 0, k + UG) if par else (half - 1, 1, k + UG)
                while k >= UG:
                    half, par, k = (half + 1, 0, k - UG) if par else (half, 1, k - UG)
                self.half, self.par, self.l, self.j = half, par, k // TG, k % TG
                self.group = 2 * half + par
                self.no = 2 * UG * half + UG * par + k
                self.ring = k % 2

            def exists(self):
                return not isinstance(self.no, int) or self.no >= 0

            def source(self):
                return x_sb[self.par][:, self.j, :] if self.l == 0 else h_sb[self.l - 1][:, self.j, :]

            def target(self):
                return h_sb[self.l][:, self.j, :] if self.l < L - 1 else o_sb[self.par][:, self.j, :]

        TAIL = [(NG // 2, NG % 2, TG * l) for l in range(L)]

        def tail_unit(l):
            u = Unit(NG // 2, NG % 2, TG * l)
            u.no = NU + l
            u.ring = l % 2
            return u

        def all_groups(eng, group):
            group(0, 0)
            with eng.Fori(0, (NG - 3) // 2) as i:
                group(i, 1)
                group(i + 1, 0)
            group((NG - 3) // 2, 1)
            group((NG - 1) // 2, 0)

        def group_view(dram, first_row):
            return dram[bass.ds(first_row, GROUP), :].rearrange("(p j) d -> p j d", j=TG)

        def sync_dense(sp):
            def load_x(half, par, group):
                sp.dma_start(x_sb[par][:], group_view(x, GROUP * group)).then_inc(x_in[par], 16)

            def group(half, par):
                u = Unit(half, par, 0)
                sp.wait_ge(h_done, u.no + TG)
                sp.dma_start(group_view(h_dram[0], GROUP * u.group), h_sb[0][:]).then_inc(h_stored[0], 16)
                if isinstance(half, int) and u.group == 0:
                    pass
                else:
                    prev = Unit(half, par, -UG)
                    sp.wait_ge(summed, TG * u.group)
                    if isinstance(half, int) and u.group == NG - 1:
                        sp.dma_start(x_sb[prev.par][0:REST, 0, :], x[NG * GROUP:N, :]).then_inc(x_in[prev.par], 16)
                    else:
                        load_x(prev.half, prev.par, u.group + 1)
                    sp.wait_ge(o_done, TG * u.group)
                    sp.dma_start(group_view(out, GROUP * prev.group), o_sb[prev.par][:]).then_inc(o_stored[prev.par], 16)
                sp.wait_ge(h_done, u.no + 2 * TG)
                sp.dma_start(group_view(h_dram[1], GROUP * u.group), h_sb[1][:]).then_inc(h_stored[1], 16)

            load_x(0, 0, 0)
            load_x(0, 1, 1)
            all_groups(sp, group)
            sp.wait_ge(o_done, TG * NG)
            sp.dma_start(group_view(out, GROUP * (NG - 1)), o_sb[(NG - 1) % 2][:]).then_inc(o_stored[(NG - 1) % 2], 16)
            for l in range(L - 1):
                sp.wait_ge(h_done, NU + l + 1)
                sp.dma_start(h_dram[l][NG * GROUP:N, :], h_sb[l][0:REST, 0, :]).then_inc(h_stored[l], 16)
            sp.wait_ge(o_done, TG * NG + 1)
            sp.dma_start(out[NG * GROUP:N, :], o_sb[NG % 2][0:REST, 0, :]).then_inc(o_stored[NG % 2], 16)
            for l in range(L - 1):
                sp.wait_ge(h_stored[l], 16 * (NG + 1))
            sp.wait_ge(o_stored[0], 16 * (-(-NG // 2)))
            sp.wait_ge(o_stored[1], 16 * (NG // 2 + 1))

        def mm3(pe, acc, aT_hi, aT_lo, w, start, stop):
            for k in range(KC):
                for a, ww in ((aT_hi, w_hi[w]), (aT_hi, w_lo[w]), (aT_lo, w_hi[w])):
                    mm = pe.matmul(acc[:], a[:, k, :], ww[:, k, :], start=start, stop=stop and k == KC - 1 and a is aT_lo)
                    start = False
            return mm

        def tensor_dense(pe):
            def turn(u, needs):
                if u.l == 0:
                    pe.wait_ge(x_in[u.par], 16 * (u.half + 1))
                else:
                    pe.wait_ge(h_done, u.no - needs + 1)
                reach(pe, low, u.no - 1)
                for k in range(KC):
                    mm = pe.transpose(ps_t[u.ring][:, k * P:(k + 1) * P], u.source()[:, k * P:(k + 1) * P], ident[:])
                mm.then_inc(turned, 1)

            def product(u):
                reach(pe, gained, u.no - 1)
                pe.matmul(ps_z[u.ring][:], ones2[:], bias2[:, u.l, :], start=True, stop=False)
                pe.wait_ge(low, u.no + 1)
                mm3(pe, ps_z[u.ring], hT_hi[u.ring], hT_lo[u.ring], u.l, False, True).then_inc(z_ready, 1)

            def group(half, par):
                for k in range(UG):
                    u = Unit(half, par, k + 1)
                    if not (isinstance(u.no, int) and u.no > NU):
                        turn(u, TG)
                    product(Unit(half, par, k))

            turn(Unit(0, 0, 0), TG)
            all_groups(pe, group)
            for l in range(L):
                if l > 0:
                    turn(tail_unit(l), 1)
                product(tail_unit(l))

        def scalar_dense(act):
            def take_high(u):
                act.wait_ge(turned, u.no + 1)
                reach(act, z_ready, u.no - 1)
                nc.scalar.copy(flat(hT_hi[u.ring]), ps_t[u.ring][:]).then_inc(high, 1)

            def scale(u):
                act.wait_ge(gained, u.no + 1)
                act.wait_ge(rstd_done, u.no + 1)
                nc.scalar.activation(y[u.ring][:], y[u.ring][:], ACT.Identity, scale=rstd[u.ring][:, 0:1]).then_inc(scaled, 1)

            def part(u):
                act.wait_ge(shifted, u.no + 1)
                reach(act, h_done, u.no - 1)
                nc.scalar.activation(pos[u.ring][:], y[u.ring][:], ACT.Relu)
                nc.scalar.activation(y[u.ring][:], y[u.ring][:], ACT.Relu, scale=-1.0).then_inc(parted, 1)

            def group(half, par):
                for k in range(UG):
                    take_high(Unit(half, par, k + 1))
                    for stage_, back in ((part, 2), (scale, 1)):
                        u = Unit(half, par, k - back)
                        if u.exists():
                            stage_(u)

            take_high(Unit(0, 0, 0))
            all_groups(act, group)
            last = Unit(NG // 2, NG % 2, -1)
            part(Unit(NG // 2, NG % 2, -2))
            scale(last)
            part(last)
            for l in range(L):
                u = tail_unit(l)
                if l > 0:
                    take_high(u)
                scale(u)
                part(u)

        def gpsimd_dense(pool):
            def rsqrt(u):
                pool.wait_ge(mv_done, u.no + 1)
                reach(pool, scaled, u.no - 1)
                pool.sem_inc(passed["pool"], 1)
                nc.gpsimd.tensor_scalar(veps[u.ring][:], mv[u.ring][:, 1:2], EPS, None, ALU.add).then_inc(veps_done, 1)
                pool.wait_ge(veps_done, u.no + 1)
                nc.gpsimd.tensor_tensor(rstd[u.ring][:], veps[u.ring][:], minus_half[:], ALU.pow).then_inc(rstd_done, 1)

            def add_shift(u):
                pool.wait_ge(scaled, u.no + 1)
                nc.gpsimd.tensor_tensor(y[u.ring][:], y[u.ring][:], shift[:, u.l, :], ALU.add).then_inc(shifted, 1)

            def out_rsqrt(n, ring):
                pool.wait_ge(omv_done, n + 1)
                pool.sem_inc(passed["pool"], 1)
                nc.gpsimd.tensor_scalar(oveps[ring][:], omv[ring][:, 1:2], EPS, None, ALU.add).then_inc(oveps_done, 1)
                pool.wait_ge(oveps_done, n + 1)
                nc.gpsimd.tensor_tensor(orstd[ring][:], oveps[ring][:], minus_half[:], ALU.pow).then_inc(orstd_done, 1)

            def group(half, par):
                for k in range(UG):
                    u = Unit(half, par, k - 1)
                    if u.exists():
                        rsqrt(u)
                        add_shift(u)
                    prev = Unit(half, par, -UG)
                    if k % 2 == 0 and k // 2 < TG and prev.exists():
                        out_rsqrt(TG * prev.group + k // 2, k // 2 % 2)

            all_groups(pool, group)
            last = Unit(NG // 2, NG % 2, -1)
            rsqrt(last)
            add_shift(last)
            for j in range(TG):
                out_rsqrt(TG * (NG - 1) + j, j % 2)
            for l in range(L):
                rsqrt(tail_unit(l))
                add_shift(tail_unit(l))
            out_rsqrt(TG * NG, 0)

        def vector_dense(dve):
            def take_low(u):
                dve.wait_ge(high, u.no + 1)
                reach(dve, z_ready, u.no - 1)
                nc.vector.tensor_tensor(flat(hT_lo[u.ring]), ps_t[u.ring][:],
                                        flat(hT_hi[u.ring]).bitcast(F32),
                                        ALU.subtract).then_inc(low, 1)

            def normal(u):
                dve.wait_ge(z_ready, u.no + 1)
                nc.vector.bn_stats(stats[u.ring][:], ps_z[u.ring][:]).then_inc(stat_done, 1)
                dve.wait_ge(stat_done, u.no + 1)
                reach(dve, parted, u.no - 1)
                dve.sem_inc(passed["dve"], 1)
                nc.vector.bn_aggr(mv[u.ring][:], stats[u.ring][:]).then_inc(mv_done, 1)
                dve.wait_ge(mv_done, u.no + 1)
                nc.vector.scalar_tensor_tensor(y[u.ring][:], ps_z[u.ring][:], mv[u.ring][:, 0:1], gain[:, u.l, :],
                                               ALU.subtract, ALU.mult).then_inc(gained, 1)

            def prelu(u, turned_before):
                dve.wait_ge(parted, u.no + 1)
                if u.l < L - 1:
                    reach(dve, turned, turned_before)
                    reach(dve, h_stored[u.l], 16 * u.group)
                else:
                    reach(dve, o_stored[u.par], 16 * u.half)
                nc.vector.scalar_tensor_tensor(u.target(), y[u.ring][:], minus_slope[:, 0:1], pos[u.ring][:],
                                               ALU.mult, ALU.add).then_inc(h_done, 1)

            def out_sum(par, j, n, done):
                dve.wait_ge(h_done, done)
                o = o_sb[par][:, j, :]
                nc.vector.tensor_tensor(o, o, x_sb[par][:, j, :], ALU.add).then_inc(summed, 1)
                dve.wait_ge(summed, n + 1)
                nc.vector.bn_stats(ostats[:], o).then_inc(ostat_done, 1)
                dve.wait_ge(ostat_done, n + 1)
                dve.sem_inc(passed["dve"], 1)
                nc.vector.bn_aggr(omv[j % 2][:], ostats[:]).then_inc(omv_done, 1)

            def out_norm(par, j, n):
                dve.wait_ge(orstd_done, n + 1)
                o = o_sb[par][:, j, :]
                nc.vector.tensor_scalar(o, o, omv[j % 2][:, 0:1], orstd[j % 2][:, 0:1],
                                        ALU.subtract, ALU.mult).then_inc(o_done, 1)

            def group(half, par):
                for k in range(UG):
                    u = Unit(half, par, k - 1)
                    if u.exists():
                        normal(u)
                    take_low(Unit(half, par, k + 1))
                    u = Unit(half, par, k - 2)
                    if u.exists():
                        prelu(u, u.no - UG + TG + 1)
                    prev = Unit(half, par, -UG)
                    if k < 2 * TG and prev.exists():
                        j = k // 2
                        n = TG * prev.group + j
                        if k % 2 == 0:
                            out_sum(prev.par, j, n, prev.no + (L - 1) * TG + j + 1)
                        else:
                            out_norm(prev.par, j, n)

            take_low(Unit(0, 0, 0))
            all_groups(dve, group)
            last = Unit(NG // 2, NG % 2, -1)
            normal(last)
            prelu(Unit(NG // 2, NG % 2, -2), NU)
            prelu(last, NU)
            for j in range(TG):
                n = TG * (NG - 1) + j
                out_sum((NG - 1) % 2, j, n, NU)
                out_norm((NG - 1) % 2, j, n)
            for l in range(L):
                u = tail_unit(l)
                if l > 0:
                    take_low(u)
                normal(u)
                prelu(u, NU)
            out_sum(NG % 2, 0, TG * NG, UNITS)
            out_norm(NG % 2, 0, TG * NG)

        with nc.Block() as block:
            block.sync(sync_dense)
            block.tensor(tensor_dense)
            block.scalar(scalar_dense)
            block.gpsimd(gpsimd_dense)
            block.vector(vector_dense)

        m_in = [h_sb[0][:, i, :] for i in range(AB)]
        self_in = [h_sb[1][:, i, :] for i in range(AB)]
        xe_in = [x_sb[0][:, i, :] for i in range(AB)]
        res = [o_sb[0][:, i, :] for i in range(AB)]
        sumT = [o_sb[1][:, i, :] for i in range(2)]
        z_sb = [o_sb[1][:, 2 + i, :] for i in range(2)]
        carried = [x_sb[1][:, i, 0:P] for i in range(2)]
        NB = ET // AB

        m_landed = [sem(f"m_landed{i}") for i in range(AB)]
        self_landed = [sem(f"self_landed{i}") for i in range(AB)]
        xe_landed = [sem(f"xe_landed{i}") for i in range(AB)]
        scattered = [sem(f"scattered{i}") for i in range(AB)]
        e_rows = sem("e_rows")
        e_xrows = sem("e_xrows")
        e_srows = sem("e_srows")
        e_turned = sem("e_turned")
        e_summed = sem("e_summed")
        e_z_ready = sem("e_z_ready")
        e_a_ready = sem("e_a_ready")
        e_high = sem("e_high")
        e_shigh = sem("e_shigh")
        e_mhigh = sem("e_mhigh")
        e_mean = sem("e_mean")
        e_scaled = sem("e_scaled")
        e_parted = sem("e_parted")
        e_z_sum = sem("e_z_sum")
        e_low = sem("e_low")
        e_mlow = sem("e_mlow")
        e_carry = sem("e_carry")
        e_slow = sem("e_slow")
        e_same = sem("e_same")
        e_stat = sem("e_stat")
        e_mv = sem("e_mv")
        e_gained = sem("e_gained")
        e_h = sem("e_h")
        e_osum = sem("e_osum")
        e_ostat = sem("e_ostat")
        e_omv = sem("e_omv")
        e_o = sem("e_o")
        e_veps = sem("e_veps")
        e_rstd = sem("e_rstd")
        e_shifted = sem("e_shifted")
        e_oveps = sem("e_oveps")
        e_orstd = sem("e_orstd")

        class Edges:

            def __init__(self, l, body, k):
                body, k = body + k // AB, k % AB
                self.l, self.body = l, body
                self.t = AB * body + k
                self.no = ET * l + self.t
                self.r4, self.r2 = k, k % 2
                self.use = NB * l + body

            def exists(self):
                return not isinstance(self.t, int) or 0 <= self.t < ET

        def all_tiles(eng, slot):
            for l in range(L):
                for k in range(-3, 2 * AB):
                    slot(l, 0, k)
                if NB > 3:
                    with eng.Fori(2, NB - 1) as body:
                        for k in range(AB):
                            slot(l, body, k)
                if NB > 2:
                    for k in range(AB):
                        slot(l, NB - 1, k)
                for k in range(6):
                    slot(l, NB, k)

        def steps(l, body, k, *todo):
            for step_, ahead in todo:
                v = Edges(l, body, k + ahead)
                if v.exists():
                    step_(v)

        def h_in(l):
            return x if l == 0 else h_dram[l - 1]

        def gpsimd_edges(pool):
            def gather(v):
                if isinstance(v.t, int) and v.t == 0 and v.l > 0:
                    for i in range(AB):
                        pool.wait_ge(scattered[i], 16 * NB * v.l)
                reach(pool, m_landed[v.r4], 16 * v.use)
                reach(pool, self_landed[v.r4], 16 * v.use)
                pool.sem_inc(passed["pool"], 1)
                nc.gpsimd.tensor_copy(gather_rows[v.r4][:], tile_rows(v, 0, 2)).then_inc(e_rows, 1)
                pool.wait_ge(e_rows, v.no + 1)
                reach(pool, e_mlow, v.no - AB + 1)
                pool.sem_inc(passed["pool"], 1)
                pool.indirect_dma_start(m_in[v.r4], None, h_in(v.l),
                                        bass.IndirectOffsetOnAxis(gather_rows[v.r4][:, 0:1], 0)).then_inc(m_landed[v.r4], 16)
                reach(pool, e_turned, v.no - AB + 1)
                pool.sem_inc(passed["pool"], 1)
                pool.indirect_dma_start(self_in[v.r4], None, h_in(v.l),
                                        bass.IndirectOffsetOnAxis(gather_rows[v.r4][:, 1:2], 0)).then_inc(self_landed[v.r4], 16)

            def gather_x(v):
                if v.l < L - 1:
                    return
                n = v.no - ET * (L - 1)
                reach(pool, xe_landed[v.r4], 16 * v.body)
                pool.sem_inc(passed["pool"], 1)
                nc.gpsimd.tensor_copy(x_rows[v.r4][:], tile_rows(v, 1, 2)).then_inc(e_xrows, 1)
                pool.wait_ge(e_xrows, n + 1)
                reach(pool, e_osum, n - AB + 1)
                pool.sem_inc(passed["pool"], 1)
                pool.indirect_dma_start(xe_in[v.r4], None, x,
                                        bass.IndirectOffsetOnAxis(x_rows[v.r4][:, 0:1], 0)).then_inc(xe_landed[v.r4], 16)

            def rsqrt(v):
                pool.wait_ge(e_mv, v.no + 1)
                reach(pool, e_scaled, v.no - 1)
                pool.sem_inc(passed["pool"], 1)
                nc.gpsimd.tensor_scalar(veps[v.r2][:], mv[v.r2][:, 1:2], EPS, None, ALU.add).then_inc(e_veps, 1)
                pool.wait_ge(e_veps, v.no + 1)
                nc.gpsimd.tensor_tensor(rstd[v.r2][:], veps[v.r2][:], minus_half[:], ALU.pow).then_inc(e_rstd, 1)

            def add_shift(v):
                pool.wait_ge(e_scaled, v.no + 1)
                nc.gpsimd.tensor_tensor(y[v.r2][:], y[v.r2][:], shift[:, v.l, :], ALU.add).then_inc(e_shifted, 1)

            def out_rsqrt(v):
                if v.l < L - 1:
                    return
                n = v.no - ET * (L - 1)
                pool.wait_ge(e_omv, n + 1)
                pool.sem_inc(passed["pool"], 1)
                nc.gpsimd.tensor_scalar(oveps[v.r2][:], omv[v.r2][:, 1:2], EPS, None, ALU.add).then_inc(e_oveps, 1)
                pool.wait_ge(e_oveps, n + 1)
                nc.gpsimd.tensor_tensor(orstd[v.r2][:], oveps[v.r2][:], minus_half[:], ALU.pow).then_inc(e_orstd, 1)

            def scatter(v, ready, count):
                reach(pool, scattered[v.r4], 16 * v.use)
                pool.sem_inc(passed["pool"], 1)
                nc.gpsimd.tensor_copy(scatter_rows[v.r4][:], tile_rows(v, 2, 3)).then_inc(e_srows, 1)
                pool.wait_ge(e_srows, v.no + 1)
                pool.wait_ge(ready, count)
                pool.sem_inc(passed["pool"], 1)
                pool.indirect_dma_start(out if v.l == L - 1 else h_dram[v.l],
                                        bass.IndirectOffsetOnAxis(scatter_rows[v.r4][:, 0:1], 0), res[v.r4], None,
                                        bounds_check=N - 1, oob_is_err=False).then_inc(scattered[v.r4], 16)

            def scatter_h(v):
                if v.l < L - 1:
                    scatter(v, e_h, v.no + 1)

            def scatter_out(v):
                if v.l == L - 1:
                    scatter(v, e_o, v.no - ET * (L - 1) + 1)

            def slot(l, body, k):
                steps(l, body, k, (gather, 3), (gather_x, -1), (rsqrt, -1), (add_shift, -1),
                      (scatter_h, -3), (out_rsqrt, -3), (scatter_out, -5))

            all_tiles(pool, slot)
            for i in range(AB):
                pool.wait_ge(scattered[i], 16 * NB * L)

        def tile_rows(v, c0, c1):
            return rows_of[:, bass.ds(v.t, 1), c0:c1].rearrange("p a c -> p (a c)")

        def tensor_edges(pe):
            def turn(v):
                pe.wait_ge(self_landed[v.r4], 16 * (v.use + 1))
                reach(pe, e_low, v.no - 1)
                for k in range(KC):
                    mm = pe.transpose(ps_t[v.r2][:, k * P:(k + 1) * P], self_in[v.r4][:, k * P:(k + 1) * P], ident[:])
                mm.then_inc(e_turned, 1)

            def sum_messages(v):
                pe.wait_ge(e_same, v.no + 1)
                pe.wait_ge(e_mlow, v.no + 1)
                reach(pe, e_carry, v.no - 1)
                for k in range(KC):
                    pe.matmul(ps_s[v.r2][:, k * P:(k + 1) * P], m_hi[v.r2][:, k * P:(k + 1) * P], same[v.r2][:],
                              start=True, stop=False)
                    mm = pe.matmul(ps_s[v.r2][:, k * P:(k + 1) * P], m_lo[v.r2][:, k * P:(k + 1) * P], same[v.r2][:],
                                   start=False, stop=True)
                mm.then_inc(e_summed, 1)

            def product(v):
                reach(pe, e_z_sum, v.no - 1)
                pe.matmul(ps_z[v.r2][:], ones2[:], bias2[:, v.l, :], start=True, stop=False)
                pe.wait_ge(e_low, v.no + 1)
                mm3(pe, ps_z[v.r2], hT_hi[v.r2], hT_lo[v.r2], v.l, False, True).then_inc(e_z_ready, 1)
                pe.wait_ge(e_slow, v.no + 1)
                mm3(pe, ps_a[v.r2], sT_hi[v.r2], sT_lo[v.r2], L + v.l, True, True).then_inc(e_a_ready, 1)

            def slot(l, body, k):
                steps(l, body, k, (sum_messages, 1), (turn, 1), (product, 0))

            all_tiles(pe, slot)

        def scalar_edges(act):
            def mean(v):
                act.wait_ge(e_a_ready, v.no + 1)
                reach(act, e_gained, v.no - 1)
                nc.scalar.activation(z_sb[v.r2], ps_a[v.r2][:], ACT.Identity,
                                     scale=rcount[:, bass.ds(v.t, 1)]).then_inc(e_mean, 1)

            def take_high(v):
                act.wait_ge(e_turned, v.no + 1)
                reach(act, e_z_ready, v.no - 1)
                nc.scalar.copy(flat(hT_hi[v.r2]), ps_t[v.r2][:]).then_inc(e_high, 1)

            def take_sum_high(v):
                act.wait_ge(e_carry, v.no + 1)
                reach(act, e_a_ready, v.no - 1)
                nc.scalar.copy(flat(sT_hi[v.r2]), sumT[v.r2]).then_inc(e_shigh, 1)

            def take_message_high(v):
                act.wait_ge(m_landed[v.r4], 16 * (v.use + 1))
                reach(act, e_summed, v.no - 1)
                nc.scalar.copy(m_hi[v.r2][:], m_in[v.r4]).then_inc(e_mhigh, 1)

            def part(v):
                act.wait_ge(e_shifted, v.no + 1)
                reach(act, e_h, v.no - 1)
                nc.scalar.activation(pos[v.r2][:], y[v.r2][:], ACT.Relu)
                nc.scalar.activation(y[v.r2][:], y[v.r2][:], ACT.Relu, scale=-1.0).then_inc(e_parted, 1)

            def scale(v):
                act.wait_ge(e_gained, v.no + 1)
                act.wait_ge(e_rstd, v.no + 1)
                nc.scalar.activation(y[v.r2][:], y[v.r2][:], ACT.Identity, scale=rstd[v.r2][:, 0:1]).then_inc(e_scaled, 1)

            def slot(l, body, k):
                steps(l, body, k, (mean, -1), (take_high, 1), (take_sum_high, 1), (take_message_high, 2),
                      (part, -2), (scale, -1))

            all_tiles(act, slot)

        def vector_edges(dve):
            def add_products(v):
                dve.wait_ge(e_mean, v.no + 1)
                nc.vector.tensor_tensor(z_sb[v.r2], z_sb[v.r2], ps_z[v.r2][:], ALU.add).then_inc(e_z_sum, 1)

            def take_low(v):
                dve.wait_ge(e_high, v.no + 1)
                nc.vector.tensor_tensor(flat(hT_lo[v.r2]), ps_t[v.r2][:], flat(hT_hi[v.r2]).bitcast(F32),
                                        ALU.subtract).then_inc(e_low, 1)

            def carry(v):
                dve.wait_ge(e_summed, v.no + 1)
                reach(dve, e_slow, v.no - 1)
                if isinstance(v.t, int) and v.t == 0:
                    nc.vector.tensor_copy(sumT[v.r2], ps_s[v.r2][:]).then_inc(e_carry, 1)
                    return
                dve.wait_ge(e_carry, v.no)
                for k in range(KC):
                    ins = nc.vector.scalar_tensor_tensor(
                        sumT[v.r2][:, k * P:(k + 1) * P], carried[v.r2],
                        sumT[1 - v.r2][:, (k + 1) * P - 1:(k + 1) * P],
                        ps_s[v.r2][:, k * P:(k + 1) * P], ALU.mult, ALU.add)
                ins.then_inc(e_carry, 1)

            def take_sum_low(v):
                dve.wait_ge(e_shigh, v.no + 1)
                nc.vector.tensor_tensor(flat(sT_lo[v.r2]), sumT[v.r2], flat(sT_hi[v.r2]).bitcast(F32),
                                        ALU.subtract).then_inc(e_slow, 1)

            def normal(v):
                dve.wait_ge(e_z_sum, v.no + 1)
                nc.vector.bn_stats(stats[v.r2][:], z_sb[v.r2]).then_inc(e_stat, 1)
                dve.wait_ge(e_stat, v.no + 1)
                reach(dve, e_parted, v.no - 1)
                dve.sem_inc(passed["dve"], 1)
                nc.vector.bn_aggr(mv[v.r2][:], stats[v.r2][:]).then_inc(e_mv, 1)
                dve.wait_ge(e_mv, v.no + 1)
                nc.vector.scalar_tensor_tensor(y[v.r2][:], z_sb[v.r2], mv[v.r2][:, 0:1], gain[:, v.l, :],
                                               ALU.subtract, ALU.mult).then_inc(e_gained, 1)

            def compare(v):
                reach(dve, e_summed, v.no - 1)
                reach(dve, e_carry, v.no - 1)
                here = dst_row[:, bass.ds(v.t * P + 1, P)]
                if not (isinstance(v.t, int) and v.t == 0):
                    nc.vector.tensor_scalar(carried[v.r2], here, dst_row[:, bass.ds(v.t * P, 1)], None, ALU.is_equal)
                nc.vector.tensor_scalar(same[v.r2][:], here, dst_col[:, bass.ds(v.t, 1)], None,
                                        ALU.is_equal).then_inc(e_same, 1)

            def take_message_low(v):
                dve.wait_ge(e_mhigh, v.no + 1)
                nc.vector.tensor_tensor(m_lo[v.r2][:], m_in[v.r4], m_hi[v.r2][:].bitcast(F32),
                                        ALU.subtract).then_inc(e_mlow, 1)

            def prelu(v):
                dve.wait_ge(e_parted, v.no + 1)
                reach(dve, scattered[v.r4], 16 * v.use)
                nc.vector.scalar_tensor_tensor(res[v.r4], y[v.r2][:], minus_slope[:, 0:1], pos[v.r2][:],
                                               ALU.mult, ALU.add).then_inc(e_h, 1)

            def out_sum(v):
                if v.l < L - 1:
                    return
                n = v.no - ET * (L - 1)
                dve.wait_ge(xe_landed[v.r4], 16 * (v.body + 1))
                dve.wait_ge(e_h, v.no + 1)
                nc.vector.tensor_tensor(res[v.r4], res[v.r4], xe_in[v.r4], ALU.add).then_inc(e_osum, 1)
                dve.wait_ge(e_osum, n + 1)
                nc.vector.bn_stats(ostats[:], res[v.r4]).then_inc(e_ostat, 1)
                dve.wait_ge(e_ostat, n + 1)
                dve.sem_inc(passed["dve"], 1)
                nc.vector.bn_aggr(omv[v.r2][:], ostats[:]).then_inc(e_omv, 1)

            def out_norm(v):
                if v.l < L - 1:
                    return
                dve.wait_ge(e_orstd, v.no - ET * (L - 1) + 1)
                nc.vector.tensor_scalar(res[v.r4], res[v.r4], omv[v.r2][:, 0:1], orstd[v.r2][:, 0:1],
                                        ALU.subtract, ALU.mult).then_inc(e_o, 1)

            def slot(l, body, k):
                steps(l, body, k, (add_products, -1), (take_low, 1), (carry, 1), (take_sum_low, 1), (normal, -1),
                      (compare, 2), (take_message_low, 2), (prelu, -2), (out_sum, -3), (out_norm, -4))

            all_tiles(dve, slot)

        with nc.Block() as block:
            block.gpsimd(gpsimd_edges)
            block.tensor(tensor_edges)
            block.scalar(scalar_edges)
            block.vector(vector_edges)


def flat(t):
    return t[:].rearrange("p k n -> p (k n)")


def kernel(**inputs):
    import concourse.bacc as bacc
    from concourse.bass_utils import run_bass_kernel_spmd

    nc = bacc.Bacc("TRN2", target_bir_lowering=False, num_devices=1)
    arrays = {}

    def given(name, array):
        array = np.ascontiguousarray(array)
        arrays[f"in_{name}"] = array
        return nc.dram_tensor(f"in_{name}", array.shape, mybir.dt.from_np(array.dtype), kind="ExternalInput").ap()

    N = inputs["x"].shape[0]
    E = inputs["src"].shape[0]
    ET = -(-E // P)
    per_layer = lambda name: [given(f"{name}{l}", inputs[f"L0_gnn_{name}{l}"]) for l in range(L)]
    ident = given("ident", np.eye(P, dtype=np.float32))
    edge_no = given("edge_no", np.arange(ET * P, dtype=np.float32).reshape(ET, P))
    row_select = given("row_select", np.eye(2, dtype=np.float32))
    dst_pad = given("dst_pad", np.array([-1] + [N] * (ET * P - E + 1), np.int32))
    src_pad = given("src_pad", np.zeros(P, np.int32))
    x = given("x", inputs["x"])
    out = nc.dram_tensor("out", x.shape, F32, kind="ExternalOutput").ap()
    build_program(nc, x, given("src", inputs["src"]), given("dst", inputs["dst"]),
                  per_layer("Wl"), per_layer("bl"), per_layer("Wr"), per_layer("g"), per_layer("b"),
                  given("a_prelu", inputs["L0_gnn_a_prelu"]), ident, edge_no, row_select, dst_pad, src_pad, out)
    result = run_bass_kernel_spmd(nc, [arrays], core_ids=[0])
    return result.results[0]["out"]
```

```python
from contextlib import ExitStack

import numpy as np

import concourse.bass as bass
from concourse import mybir

P = 128
ALU = mybir.AluOpType
ACT = mybir.ActivationFunctionType
F32 = mybir.dt.float32
F32R = mybir.dt.float32r
I32 = mybir.dt.int32
I16 = mybir.dt.int16

L = 3
TG = 4
UG = L * TG
EPS = 1e-5
FAR = 65536.0


def reach(eng, sem, count):
    if isinstance(count, int) and count <= 0:
        return
    eng.wait_ge(sem, count)


def build_program(nc, x, src, dst, Wl, bl, Wr, g, b, a_prelu, ident_in, edge_no_in, row_select_in,
                  dst_pad_in, src_pad_in, out):
    N, D = x.shape
    E = src.shape[0]
    KC = D // P
    GROUP = TG * P
    NG = N // GROUP
    REST = N - NG * GROUP
    ET = -(-E // P)
    EP = ET * P
    AB = 4
    assert N < 2 ** 15 and D == 512 and NG % 2 == 1 and NG >= 5 and 0 < REST <= P and ET % AB == 0 and ET >= 2 * AB
    NU = UG * NG
    UNITS = NU + L

    h_dram = [nc.dram_tensor(f"h{l + 1}_scratch", [N, D], F32).ap() for l in range(L - 1)]
    dst_dram = nc.dram_tensor("dst_padded", [EP + 2], I32).ap()
    src_dram = nc.dram_tensor("src_padded", [EP], I32).ap()

    with ExitStack() as ctx:
        def sb(name, shape, dt=F32):
            return ctx.enter_context(nc.sbuf_tensor(name, shape, dt))

        def sem(name):
            return ctx.enter_context(nc.semaphore(name))

        w_hi = [sb(f"w_hi{i}", [P, KC, D], F32R) for i in range(2 * L)]
        w_lo = [sb(f"w_lo{i}", [P, KC, D], F32R) for i in range(2 * L)]
        bias2 = sb("bias2", [2, L, D], F32R)
        ones2 = sb("ones2", [2, P], F32R)
        gain = sb("gain", [P, L, D])
        shift = sb("shift", [P, L, D])
        slope = sb("slope", [P, 1])
        slope_less = sb("slope_less", [P, 1])
        minus_half = sb("minus_half", [P, 1])
        ident = sb("ident", [P, P])

        x_sb = [sb(f"x_sb{i}", [P, TG, D]) for i in range(2)]
        h_sb = [sb(f"h_sb{i}", [P, TG, D]) for i in range(L - 1)]
        o_sb = [sb(f"o_sb{i}", [P, TG, D]) for i in range(2)]
        hT_hi = [sb(f"hT_hi{i}", [P, KC, P], F32R) for i in range(2)]
        hT_lo = [sb(f"hT_lo{i}", [P, KC, P], F32R) for i in range(2)]
        y = [sb(f"y{i}", [P, D]) for i in range(2)]
        neg = [sb(f"neg{i}", [P, D]) for i in range(2)]
        stats = [sb(f"stats{i}", [P, 6]) for i in range(2)]
        mv = [sb(f"mv{i}", [P, 2]) for i in range(2)]
        veps = [sb(f"veps{i}", [P, 1]) for i in range(2)]
        rstd = [sb(f"rstd{i}", [P, 1]) for i in range(2)]
        ostats = [sb(f"ostats{i}", [P, 6]) for i in range(2)]
        omv = [sb(f"omv{i}", [P, 2]) for i in range(2)]
        oveps = [sb(f"oveps{i}", [P, 1]) for i in range(2)]
        omean = [sb(f"omean{i}", [P, 1]) for i in range(2)]
        orstd = [sb(f"orstd{i}", [P, 1]) for i in range(2)]

        dst_row = sb("dst_row", [P, EP + 1], I16)
        rows_of = sb("rows_of", [P, ET, 3], I32)
        rcount = sb("rcount", [P, ET])
        dst_col = sb("dst_col", [P, ET])
        gather_rows = [sb(f"gather_rows{i}", [P, 2], I32) for i in range(AB)]
        scatter_rows = [sb(f"scatter_rows{i}", [P, 1], I32) for i in range(AB)]

        dense_only = ExitStack()
        rest_x, rest_h1, rest_h2, rest_out = [
            dense_only.enter_context(nc.sbuf_tensor(f"rest_{name}", [P, D], F32)) for name in ("x", "h1", "h2", "out")]

        ps = [ctx.enter_context(nc.psum_tensor(f"ps{i}", [P, D], F32)) for i in range(8)]
        ps_t, ps_z, ps_a, ps_s = ps[0:2], ps[2:4], ps[4:6], ps[6:8]

        passed = {e: sem(f"passed_{e}") for e in ("dve", "pool")}

        stage = [o_sb[0], o_sb[1], h_sb[0], h_sb[1]]
        WORDER = [("r", l) for l in range(L)] + [("l", l) for l in range(L)]

        with ExitStack() as sctx:
            def ssb(name, shape, dt=F32):
                return sctx.enter_context(nc.sbuf_tensor(name, shape, dt))

            def ssem(name):
                return sctx.enter_context(nc.semaphore(name))

            room, room2 = [t[:].rearrange("p j d -> p (j d)") for t in x_sb]
            lists = room[0:ET, 0:4 * P].bitcast(I32).rearrange("t (c p) -> t c p", c=4)
            listf = room[0:ET, 4 * P:8 * P].rearrange("t (c p) -> t c p", c=4)
            cols = room[0:ET, 8 * P:13 * P].rearrange("t (c p) -> t c p", c=5)
            edge_no = room[0:ET, 13 * P:14 * P]
            first = room[0:ET, 14 * P:15 * P]
            run = room[0:ET, 15 * P:16 * P]
            bias_raw = room2[0:2, 0:L * D]
            last_run = room2[0:ET, L * D:L * D + 1]
            before = room2[0:ET, L * D + 1:L * D + 2]
            row_select = room2[0:2, L * D + 2:L * D + 4]
            runs_before = room2[0:1, L * D + 4:L * D + 5 + ET]
            zero_row = room2[0:1, L * D + 64:L * D + 64 + ET]
            bias_flat = bias2[:].rearrange("p l d -> p (l d)")

            w_in = [ssem(f"w_in{i}") for i in range(4)]
            ident_in_sem = ssem("ident_in_sem")
            const_in = ssem("const_in")
            lists_copied = ssem("lists_copied")
            lists_in = ssem("lists_in")
            row_in = ssem("row_in")
            w_turned = ssem("w_turned")
            w_diag = ssem("w_diag")
            w_high = ssem("w_high")
            w_low = ssem("w_low")
            prep = ssem("prep")
            sentinel = ssem("sentinel")
            small_turned = ssem("small_turned")
            run_done = ssem("run_done")

            CONSTS = 3 + 3 * L
            with nc.Block() as block:
                @block.sync
                def _(sp):
                    def load_weight(i):
                        side, l = WORDER[i]
                        w = (Wr if side == "r" else Wl)[l]
                        if i >= 4:
                            sp.wait_ge(w_turned, KC * (i - 3))
                        sp.dma_start(stage[i % 4][:], w.rearrange("(c p) k -> p c k", p=P)).then_inc(w_in[i % 4], 16)

                    sp.dma_start(ident[:], ident_in).then_inc(ident_in_sem, 16)
                    load_weight(0)
                    sp.dma_start(dst_dram[1:E + 1], dst).then_inc(lists_copied, 16)
                    sp.dma_start(dst_dram[0:1], dst_pad_in[0:1]).then_inc(lists_copied, 16)
                    sp.dma_start(dst_dram[E + 1:EP + 2], dst_pad_in[1:EP - E + 2]).then_inc(lists_copied, 16)
                    sp.dma_start(src_dram[0:E], src).then_inc(lists_copied, 16)
                    if EP > E:
                        sp.dma_start(src_dram[E:EP], src_pad_in[0:EP - E]).then_inc(lists_copied, 16)
                    load_weight(1)
                    load_weight(2)
                    sp.dma_start(edge_no, edge_no_in).then_inc(const_in, 16)
                    sp.dma_start(row_select, row_select_in).then_inc(const_in, 16)
                    sp.dma_start(slope[:], a_prelu.rearrange("(a c) -> a c", a=1).to_broadcast([P, 1])).then_inc(const_in, 16)
                    for l in range(L):
                        sp.dma_start(bias_raw[:, l * D:(l + 1) * D], bl[l].rearrange("(a d) -> a d", a=1).to_broadcast([2, D])).then_inc(const_in, 16)
                        sp.dma_start(gain[:, l, :], g[l].rearrange("(a d) -> a d", a=1).to_broadcast([P, D])).then_inc(const_in, 16)
                        sp.dma_start(shift[:, l, :], b[l].rearrange("(a d) -> a d", a=1).to_broadcast([P, D])).then_inc(const_in, 16)
                    sp.wait_ge(lists_copied, 16 * (4 + (EP > E)))
                    tiled = lambda v: v.rearrange("(t p) -> t p", p=P)
                    sp.dma_start(lists[:, 0, :], tiled(dst_dram[1:EP + 1])).then_inc(lists_in, 16)
                    sp.dma_start(lists[:, 1, :], tiled(dst_dram[2:EP + 2])).then_inc(lists_in, 16)
                    sp.dma_start(lists[:, 2, :], tiled(dst_dram[0:EP])).then_inc(lists_in, 16)
                    sp.dma_start(lists[:, 3, :], tiled(src_dram)).then_inc(lists_in, 16)
                    for i in range(3, 2 * L):
                        load_weight(i)

                @block.tensor
                def _(pe):
                    pe.wait_ge(ident_in_sem, 16)
                    for i in range(2 * L):
                        pe.wait_ge(w_in[i % 4], 16 * (i // 4 + 1))
                        for k in range(KC):
                            n = KC * i + k
                            if n >= 2:
                                pe.wait_ge(w_low, n - 1)
                            for c in range(KC):
                                mm = pe.transpose(ps_t[n % 2][:, c * P:(c + 1) * P],
                                                  stage[i % 4][:, c, k * P:(k + 1) * P], ident[:])
                            mm.then_inc(w_turned, 1)
                    pe.wait_ge(prep, 8)
                    pe.transpose(ps_z[0][0:1, 0:ET], last_run, ident[0:ET, 0:ET]).then_inc(small_turned, 1)
                    pe.wait_ge(prep, 9)
                    pe.transpose(ps_z[1][0:ET, 0:1], runs_before[0:1, 0:ET], ident[0:1, 0:1]).then_inc(small_turned, 1)
                    pe.wait_ge(prep, 16)
                    for c in range(5):
                        mm = pe.transpose(ps_a[0][:, c * ET:(c + 1) * ET], cols[:, c, :], ident[0:ET, 0:ET])
                    mm.then_inc(small_turned, 1)

                @block.scalar
                def _(act):
                    for i in range(2 * L):
                        side, l = WORDER[i]
                        for k in range(KC):
                            n = KC * i + k
                            if side == "r" and l > 0:
                                act.wait_ge(w_diag, KC * (i - 1) + k + 1)
                            else:
                                act.wait_ge(w_turned, n + 1)
                            nc.scalar.copy(w_hi[i][:, k, :], ps_t[n % 2][:]).then_inc(w_high, 1)

                @block.gpsimd
                def _(pool):
                    pool.wait_ge(lists_copied, 16 * (4 + (EP > E)))
                    pool.dma_start(dst_row[:], dst_dram[0:EP + 1].rearrange("(a d) -> a d", a=1)
                                   .to_broadcast([P, EP + 1])).then_inc(row_in, 16)
                    pool.wait_ge(row_in, 16)

                @block.vector
                def _(dve):
                    dve.wait_ge(ident_in_sem, 16)
                    nc.vector.memset(ones2[:].bitcast(F32), 1.0)
                    nc.vector.memset(minus_half[:], -0.5)
                    nc.vector.memset(runs_before[:, 0:1], 0.0)
                    nc.vector.memset(zero_row, 0.0)
                    nc.vector.memset(rest_x[:], 0.0)
                    for i in range(2 * L):
                        side, l = WORDER[i]
                        for k in range(KC):
                            n = KC * i + k
                            if side == "r" and l > 0:
                                dve.wait_ge(w_turned, n + 1)
                                diag = ps_t[n % 2][:, k * P:(k + 1) * P]
                                nc.vector.tensor_tensor(diag, diag, ident[:], ALU.add).then_inc(w_diag, 1)
                            dve.wait_ge(w_high, n + 1)
                            nc.vector.tensor_tensor(w_lo[i][:, k, :], ps_t[n % 2][:],
                                                    w_hi[i][:, k, :].bitcast(F32), ALU.subtract).then_inc(w_low, 1)

                    step = [0]

                    def then(ins):
                        step[0] += 1
                        ins.then_inc(prep, 1)
                        dve.wait_ge(prep, step[0])

                    dve.wait_ge(const_in, 16 * CONSTS)
                    then(nc.vector.tensor_copy(bias_flat, bias_raw))
                    then(nc.vector.tensor_tensor(bias_raw, bias_raw, bias_flat.bitcast(F32), ALU.subtract))
                    then(nc.vector.tensor_scalar(bias_flat, bias_flat.bitcast(F32), row_select[:, 0:1], None, ALU.mult))
                    then(nc.vector.scalar_tensor_tensor(bias_flat, bias_raw, row_select[:, 1:2], bias_flat.bitcast(F32),
                                                        ALU.mult, ALU.add))
                    dve.wait_ge(lists_in, 64)
                    then(nc.vector.tensor_copy(listf, lists))
                    then(nc.vector.tensor_tensor(first, listf[:, 0, :], listf[:, 2, :], ALU.not_equal))
                    then(nc.vector.tensor_tensor(first, first, edge_no, ALU.mult))
                    nc.vector.tensor_tensor_scan(run, first, first, 0.0, ALU.max, ALU.max).then_inc(run_done, 1)
                    dve.wait_ge(run_done, 1)
                    then(nc.vector.tensor_copy(last_run, run[:, P - 1:P]))
                    dve.wait_ge(small_turned, 1)
                    then(nc.vector.tensor_tensor_scan(runs_before[:, 1:ET + 1], ps_z[0][0:1, 0:ET], zero_row,
                                                      0.0, ALU.max, ALU.max))
                    dve.wait_ge(small_turned, 2)
                    then(nc.vector.tensor_copy(before, ps_z[1][0:ET, 0:1]))
                    then(nc.vector.tensor_scalar(run, run, before[:, 0:1], -1.0, ALU.max, ALU.mult))
                    then(nc.vector.scalar_tensor_tensor(first, edge_no, 1.0, run, ALU.add, ALU.add))
                    then(nc.vector.reciprocal(cols[:, 3, :], first))
                    nc.vector.tensor_copy(cols[:, 0, :], listf[:, 3, :])
                    nc.vector.tensor_copy(cols[:, 4, :], listf[:, 0, :])
                    then(nc.vector.tensor_scalar(cols[:, 1, :], listf[:, 0, :], float(N - 1), None, ALU.min))
                    then(nc.vector.tensor_tensor(run, listf[:, 0, :], listf[:, 1, :], ALU.is_equal))
                    then(nc.vector.scalar_tensor_tensor(cols[:, 2, :], run, FAR, listf[:, 0, :], ALU.mult, ALU.add))
                    dve.wait_ge(small_turned, 3)
                    nc.vector.tensor_copy(rows_of[:].rearrange("p t c -> p c t"),
                                          ps_a[0][:, 0:3 * ET].rearrange("p (c t) -> p c t", c=3))
                    nc.vector.tensor_copy(rcount[:], ps_a[0][:, 3 * ET:4 * ET])
                    nc.vector.tensor_copy(dst_col[:], ps_a[0][:, 4 * ET:5 * ET])
                    nc.vector.tensor_scalar(slope_less[:], slope[:], -1.0, 1.0, ALU.mult, ALU.add)

        x_in = [sem(f"x_in{i}") for i in range(2)]
        rest_in = sem("rest_in")
        turned = sem("turned")
        high = sem("high")
        low = sem("low")
        z_ready = sem("z_ready")
        stat_done = sem("stat_done")
        mv_done = sem("mv_done")
        gained = sem("gained")
        veps_done = sem("veps_done")
        rstd_done = sem("rstd_done")
        scaled = sem("scaled")
        shifted = sem("shifted")
        parted = sem("parted")
        h_done = sem("h_done")
        summed = sem("summed")
        ostat_done = sem("ostat_done")
        omv_done = sem("omv_done")
        oveps_done = sem("oveps_done")
        orstd_done = sem("orstd_done")
        omean_done = sem("omean_done")
        o_done = sem("o_done")
        h_stored = [sem(f"h_stored{i}") for i in range(L - 1)]
        o_stored = [sem(f"o_stored{i}") for i in range(2)]

        rest_h = [rest_h1, rest_h2]
        LAST_UNITS = L * (TG + 1)

        class Unit:

            def __init__(self, half, par, k):
                while k < 0:
                    half, par, k = (half, 0, k + UG) if par else (half - 1, 1, k + UG)
                while k >= UG and not self.is_last(half, par):
                    half, par, k = (half + 1, 0, k - UG) if par else (half, 1, k - UG)
                self.half, self.par, self.k = half, par, k
                self.tiles = TG + 1 if self.is_last(half, par) else TG
                self.l, self.j = k // self.tiles, k % self.tiles
                self.group = 2 * half + par
                self.base = 2 * UG * half + UG * par
                self.no = self.base + k
                self.ring = k % 2

            @staticmethod
            def is_last(half, par):
                return isinstance(half, int) and 2 * half + par == NG - 1

            def exists(self):
                return not isinstance(self.no, int) or 0 <= self.no < UNITS

            def source(self):
                if self.j == TG:
                    return rest_x[:] if self.l == 0 else rest_h[self.l - 1][:]
                return x_sb[self.par][:, self.j, :] if self.l == 0 else h_sb[self.l - 1][:, self.j, :]

            def target(self):
                if self.j == TG:
                    return rest_h[self.l][:] if self.l < L - 1 else rest_out[:]
                return h_sb[self.l][:, self.j, :] if self.l < L - 1 else o_sb[self.par][:, self.j, :]

        class Output:

            def __init__(self, half, par, j):
                self.j, self.ring = j, j % 2
                self.no = 2 * TG * half + TG * par + j
                last = Unit.is_last(half, par)
                self.units = 2 * UG * half + UG * par + (L - 1) * (TG + last) + j + 1
                self.o = rest_out[:] if j == TG else o_sb[par][:, j, :]
                self.x = rest_x[:] if j == TG else x_sb[par][:, j, :]

        def slots(half, par):
            return LAST_UNITS + 6 if Unit.is_last(half, par) else UG

        def output_steps(half, par, k, sum0=None, sum1=None, stats_=None, root=None, norm=None):
            prev = Unit(half, par, -UG)
            for step, back in ((norm, 3), (root, 2), (stats_, 2), (sum1, 1), (sum0, 0)):
                if not step:
                    continue
                first = k - back + 1
                if prev.exists() and first % 3 == 0 and k >= 0 and 0 <= first // 3 < TG:
                    step(Output(prev.half, prev.par, first // 3))
                if not Unit.is_last(half, par):
                    if k - back + 1 == UG:
                        step(Output(half, par, 0))
                else:
                    j = k - back - (L - 1) * (TG + 1) - 3
                    if 0 <= j <= TG:
                        step(Output(half, par, j))

        def all_groups(eng, group):
            group(0, 0)
            with eng.Fori(0, (NG - 3) // 2) as i:
                group(i, 1)
                group(i + 1, 0)
            group((NG - 3) // 2, 1)
            group((NG - 1) // 2, 0)

        def group_view(dram, first_row):
            return dram[bass.ds(first_row, GROUP), :].rearrange("(p j) d -> p j d", j=TG)

        def sync_dense(sp):
            def load_x(half, par, group):
                sp.dma_start(x_sb[par][:], group_view(x, GROUP * group)).then_inc(x_in[par], 16)

            def group(half, par):
                u = Unit(half, par, 0)
                sp.wait_ge(h_done, u.no + TG)
                sp.dma_start(group_view(h_dram[0], GROUP * u.group), h_sb[0][:]).then_inc(h_stored[0], 16)
                if not (isinstance(half, int) and u.group == 0):
                    prev = Unit(half, par, -UG)
                    sp.wait_ge(summed, TG * u.group)
                    if not (isinstance(half, int) and u.group == NG - 1):
                        load_x(prev.half, prev.par, u.group + 1)
                    sp.wait_ge(o_done, TG * u.group)
                    sp.dma_start(group_view(out, GROUP * prev.group), o_sb[prev.par][:]).then_inc(o_stored[prev.par], 16)
                sp.wait_ge(h_done, u.no + u.tiles + TG)
                sp.dma_start(group_view(h_dram[1], GROUP * u.group), h_sb[1][:]).then_inc(h_stored[1], 16)

            load_x(0, 0, 0)
            load_x(0, 1, 1)
            sp.dma_start(rest_x[0:REST], x[NG * GROUP:N, :]).then_inc(rest_in, 16)
            all_groups(sp, group)
            for l in range(L - 1):
                sp.wait_ge(h_done, NU - UG + (TG + 1) * (l + 1))
                sp.dma_start(h_dram[l][NG * GROUP:N, :], rest_h[l][0:REST]).then_inc(h_stored[l], 16)
            sp.wait_ge(o_done, TG * NG)
            sp.dma_start(group_view(out, GROUP * (NG - 1)), o_sb[(NG - 1) % 2][:]).then_inc(o_stored[(NG - 1) % 2], 16)
            sp.wait_ge(o_done, TG * NG + 1)
            sp.dma_start(out[NG * GROUP:N, :], rest_out[0:REST]).then_inc(o_stored[NG % 2], 16)
            for l in range(L - 1):
                sp.wait_ge(h_stored[l], 16 * (NG + 1))
            sp.wait_ge(o_stored[0], 16 * (-(-NG // 2)))
            sp.wait_ge(o_stored[1], 16 * (NG // 2 + 1))

        def mm3(pe, acc, aT_hi, aT_lo, w, start, stop, chunks=range(KC)):
            for k in chunks:
                for a, ww in ((aT_hi, w_hi[w]), (aT_hi, w_lo[w]), (aT_lo, w_hi[w])):
                    mm = pe.matmul(acc[:], a[:, k, :], ww[:, k, :], start=start, stop=stop and k == KC - 1 and a is aT_lo)
                    start = False
            return mm

        def tensor_dense(pe):
            def turn(u):
                if u.j == TG and u.l == 0:
                    pe.wait_ge(rest_in, 16)
                elif u.l == 0:
                    pe.wait_ge(x_in[u.par], 16 * (u.half + 1))
                else:
                    pe.wait_ge(h_done, u.no - u.tiles + 1)
                reach(pe, low, u.no - 1)
                for k in range(KC):
                    mm = pe.transpose(ps_t[u.ring][:, k * P:(k + 1) * P], u.source()[:, k * P:(k + 1) * P], ident[:])
                mm.then_inc(turned, 1)

            def begin_product(u):
                reach(pe, gained, u.no - 1)
                pe.matmul(ps_z[u.ring][:], ones2[:], bias2[:, u.l, :], start=True, stop=False)
                pe.wait_ge(low, u.no + 1)
                mm3(pe, ps_z[u.ring], hT_hi[u.ring], hT_lo[u.ring], u.l, False, True, range(1))

            def end_product(u):
                mm3(pe, ps_z[u.ring], hT_hi[u.ring], hT_lo[u.ring], u.l, False, True, range(1, KC)).then_inc(z_ready, 1)

            def group(half, par):
                for k in range(slots(half, par)):
                    for stage_, ahead in ((begin_product, 0), (turn, 1), (end_product, 0)):
                        u = Unit(half, par, k + ahead)
                        if u.exists():
                            stage_(u)

            turn(Unit(0, 0, 0))
            all_groups(pe, group)

        def scalar_dense(act):
            def take_high(u):
                act.wait_ge(turned, u.no + 1)
                reach(act, z_ready, u.no - 1)
                nc.scalar.copy(flat(hT_hi[u.ring]), ps_t[u.ring][:]).then_inc(high, 1)

            def scale(u):
                act.wait_ge(gained, u.no + 1)
                act.wait_ge(rstd_done, u.no + 1)
                nc.scalar.activation(y[u.ring][:], y[u.ring][:], ACT.Identity, scale=rstd[u.ring][:, 0:1]).then_inc(scaled, 1)

            def part(u):
                act.wait_ge(shifted, u.no + 1)
                reach(act, h_done, u.no - 1)
                nc.scalar.activation(neg[u.ring][:], y[u.ring][:], ACT.Relu, scale=-1.0).then_inc(parted, 1)

            def out_norm(t):
                act.wait_ge(orstd_done, t.no + 1)
                act.wait_ge(omean_done, t.no + 1)
                nc.scalar.activation(t.o, t.o, ACT.Identity, scale=orstd[t.ring][:, 0:1],
                                     bias=omean[t.ring][:, 0:1]).then_inc(o_done, 1)

            def group(half, par):
                for k in range(slots(half, par)):
                    for stage_, ahead in ((take_high, 1), (part, -2), (scale, -1)):
                        u = Unit(half, par, k + ahead)
                        if u.exists():
                            stage_(u)
                    output_steps(half, par, k, norm=out_norm)

            take_high(Unit(0, 0, 0))
            all_groups(act, group)

        def gpsimd_dense(pool):
            def rsqrt(u):
                pool.wait_ge(mv_done, u.no + 1)
                reach(pool, scaled, u.no - 1)
                pool.sem_inc(passed["pool"], 1)
                nc.gpsimd.tensor_scalar(veps[u.ring][:], mv[u.ring][:, 1:2], EPS, None, ALU.add).then_inc(veps_done, 1)
                pool.wait_ge(veps_done, u.no + 1)
                nc.gpsimd.tensor_tensor(rstd[u.ring][:], veps[u.ring][:], minus_half[:], ALU.pow).then_inc(rstd_done, 1)

            def add_shift(u):
                pool.wait_ge(scaled, u.no + 1)
                nc.gpsimd.tensor_tensor(y[u.ring][:], y[u.ring][:], shift[:, u.l, :], ALU.add).then_inc(shifted, 1)

            def out_sum_left(t):
                pool.wait_ge(h_done, t.units)
                nc.gpsimd.tensor_tensor(t.o[:, 0:D // 2], t.o[:, 0:D // 2], t.x[:, 0:D // 2], ALU.add)

            def out_sum_right(t):
                nc.gpsimd.tensor_tensor(t.o[:, D // 2:D], t.o[:, D // 2:D], t.x[:, D // 2:D], ALU.add).then_inc(summed, 1)

            def out_rsqrt(t):
                pool.wait_ge(omv_done, t.no + 1)
                if isinstance(t.no, int):
                    reach(pool, o_done, t.no - 1)
                pool.sem_inc(passed["pool"], 1)
                nc.gpsimd.tensor_scalar(oveps[t.ring][:], omv[t.ring][:, 1:2], EPS, None, ALU.add).then_inc(oveps_done, 1)
                pool.wait_ge(oveps_done, t.no + 1)
                nc.gpsimd.tensor_tensor(orstd[t.ring][:], oveps[t.ring][:], minus_half[:], ALU.pow).then_inc(orstd_done, 1)
                pool.wait_ge(orstd_done, t.no + 1)
                pool.sem_inc(passed["pool"], 1)
                nc.gpsimd.tensor_scalar(omean[t.ring][:], omv[t.ring][:, 0:1], orstd[t.ring][:, 0:1], -1.0,
                                        ALU.mult, ALU.mult).then_inc(omean_done, 1)

            def group(half, par):
                for k in range(slots(half, par)):
                    u = Unit(half, par, k - 1)
                    if u.exists():
                        rsqrt(u)
                    output_steps(half, par, k, sum0=out_sum_left, sum1=out_sum_right, root=out_rsqrt)
                    if u.exists():
                        add_shift(u)

            all_groups(pool, group)

        def vector_dense(dve):
            def take_low(u):
                dve.wait_ge(high, u.no + 1)
                reach(dve, z_ready, u.no - 1)
                nc.vector.tensor_tensor(flat(hT_lo[u.ring]), ps_t[u.ring][:],
                                        flat(hT_hi[u.ring]).bitcast(F32),
                                        ALU.subtract).then_inc(low, 1)

            def statistics(u):
                dve.wait_ge(z_ready, u.no + 1)
                nc.vector.bn_stats(stats[u.ring][:], ps_z[u.ring][:]).then_inc(stat_done, 1)

            def mean(u):
                dve.wait_ge(stat_done, u.no + 1)
                reach(dve, parted, u.no - 1)
                dve.sem_inc(passed["dve"], 1)
                nc.vector.bn_aggr(mv[u.ring][:], stats[u.ring][:]).then_inc(mv_done, 1)

            def normal(u):
                dve.wait_ge(mv_done, u.no + 1)
                nc.vector.scalar_tensor_tensor(y[u.ring][:], ps_z[u.ring][:], mv[u.ring][:, 0:1], gain[:, u.l, :],
                                               ALU.subtract, ALU.mult).then_inc(gained, 1)

            def prelu(u):
                dve.wait_ge(parted, u.no + 1)
                if u.j == TG:
                    pass
                elif u.l < L - 1:
                    reach(dve, turned, u.base + (TG * (u.l + 1) + u.j + 1 - UG))
                    reach(dve, h_stored[u.l], 16 * u.group)
                else:
                    reach(dve, o_stored[u.par], 16 * u.half)
                nc.vector.scalar_tensor_tensor(u.target(), neg[u.ring][:], slope_less[:, 0:1], y[u.ring][:],
                                               ALU.mult, ALU.add).then_inc(h_done, 1)

            def out_statistics(t):
                dve.wait_ge(summed, t.no + 1)
                nc.vector.bn_stats(ostats[t.ring][:], t.o).then_inc(ostat_done, 1)

            def out_mean(t):
                dve.wait_ge(ostat_done, t.no + 1)
                dve.sem_inc(passed["dve"], 1)
                nc.vector.bn_aggr(omv[t.ring][:], ostats[t.ring][:]).then_inc(omv_done, 1)

            def group(half, par):
                for k in range(slots(half, par)):
                    u = Unit(half, par, k - 1)
                    if u.exists():
                        statistics(u)
                    output_steps(half, par, k, stats_=out_statistics)
                    if u.exists():
                        mean(u)
                    output_steps(half, par, k, stats_=out_mean)
                    if u.exists():
                        normal(u)
                    for stage_, ahead in ((take_low, 1), (prelu, -2)):
                        u = Unit(half, par, k + ahead)
                        if u.exists():
                            stage_(u)

            take_low(Unit(0, 0, 0))
            all_groups(dve, group)

        with nc.Block() as block:
            block.sync(sync_dense)
            block.tensor(tensor_dense)
            block.scalar(scalar_dense)
            block.gpsimd(gpsimd_dense)
            block.vector(vector_dense)

        dense_only.close()
        same = [sb(f"same{i}", [P, P], F32R) for i in range(2)]
        m_hi = [sb(f"m_hi{i}", [P, D], F32R) for i in range(2)]
        m_lo = [sb(f"m_lo{i}", [P, D], F32R) for i in range(2)]
        sT_hi = [sb(f"sT_hi{i}", [P, KC, P], F32R) for i in range(2)]
        sT_lo = [sb(f"sT_lo{i}", [P, KC, P], F32R) for i in range(2)]
        m_in = [h_sb[0][:, i, :] for i in range(AB)]
        self_in = [h_sb[1][:, i, :] for i in range(AB)]
        xe_in = [x_sb[0][:, i, :] for i in range(AB)]
        res = [o_sb[0][:, i, :] for i in range(AB)]
        sumT = [o_sb[1][:, i, :] for i in range(2)]
        z_sb = [o_sb[1][:, 2 + i, :] for i in range(2)]
        carried = [x_sb[1][:, i, 0:P] for i in range(2)]
        over = [x_sb[1][:, 2 + i, :] for i in range(2)]
        NB = ET // AB

        m_landed = [sem(f"m_landed{i}") for i in range(AB)]
        self_landed = [sem(f"self_landed{i}") for i in range(AB)]
        xe_landed = [sem(f"xe_landed{i}") for i in range(AB)]
        scattered = [sem(f"scattered{i}") for i in range(AB)]
        e_rows = sem("e_rows")
        e_srows = sem("e_srows")
        e_turned = sem("e_turned")
        e_summed = sem("e_summed")
        e_z_ready = sem("e_z_ready")
        e_a_ready = sem("e_a_ready")
        e_high = sem("e_high")
        e_shigh = sem("e_shigh")
        e_mhigh = sem("e_mhigh")
        e_mean = sem("e_mean")
        e_scaled = sem("e_scaled")
        e_parted = sem("e_parted")
        e_z_sum = sem("e_z_sum")
        e_low = sem("e_low")
        e_mlow = sem("e_mlow")
        e_carry = sem("e_carry")
        e_slow = sem("e_slow")
        e_same = sem("e_same")
        e_stat = sem("e_stat")
        e_mv = sem("e_mv")
        e_gained = sem("e_gained")
        e_h = sem("e_h")
        e_osum = sem("e_osum")
        e_ostat = sem("e_ostat")
        e_omv = sem("e_omv")
        e_o = sem("e_o")
        e_veps = sem("e_veps")
        e_rstd = sem("e_rstd")
        e_shifted = sem("e_shifted")
        e_oveps = sem("e_oveps")
        e_orstd = sem("e_orstd")
        e_omean = sem("e_omean")
        e_taken_over = sem("e_taken_over")

        class Edges:

            def __init__(self, l, body, k):
                body, k = body + k // AB, k % AB
                self.l, self.body = l, body
                self.t = AB * body + k
                self.no = ET * l + self.t
                self.r4, self.r2 = k, k % 2
                self.use = NB * l + body

            def exists(self):
                return not isinstance(self.t, int) or 0 <= self.t < ET

        def all_tiles(eng, slot):
            for l in range(L):
                for k in range(-4, 2 * AB):
                    slot(l, 0, k)
                if NB > 3:
                    with eng.Fori(2, NB - 1) as body:
                        for k in range(AB):
                            slot(l, body, k)
                if NB > 2:
                    for k in range(AB):
                        slot(l, NB - 1, k)
                for k in range(6):
                    slot(l, NB, k)

        def steps(l, body, k, *todo):
            for step_, ahead in todo:
                v = Edges(l, body, k + ahead)
                if v.exists():
                    step_(v)

        def h_in(l):
            return x if l == 0 else h_dram[l - 1]

        def gpsimd_edges(pool):
            def gather(v):
                if isinstance(v.t, int) and v.t == 0 and v.l > 0:
                    for i in range(AB):
                        pool.wait_ge(scattered[i], 16 * NB * v.l)
                reach(pool, m_landed[v.r4], 16 * v.use)
                reach(pool, self_landed[v.r4], 16 * v.use)
                if v.l == L - 1:
                    reach(pool, xe_landed[v.r4], 16 * v.body)
                pool.sem_inc(passed["pool"], 1)
                nc.gpsimd.tensor_copy(gather_rows[v.r4][:], tile_rows(v, 0, 2)).then_inc(e_rows, 1)
                pool.wait_ge(e_rows, v.no + 1)
                reach(pool, e_mlow, v.no - AB + 1)
                pool.sem_inc(passed["pool"], 1)
                pool.indirect_dma_start(m_in[v.r4], None, h_in(v.l),
                                        bass.IndirectOffsetOnAxis(gather_rows[v.r4][:, 0:1], 0)).then_inc(m_landed[v.r4], 16)
                reach(pool, e_turned, v.no - AB + 1)
                pool.sem_inc(passed["pool"], 1)
                pool.indirect_dma_start(self_in[v.r4], None, h_in(v.l),
                                        bass.IndirectOffsetOnAxis(gather_rows[v.r4][:, 1:2], 0)).then_inc(self_landed[v.r4], 16)

            def gather_x(v):
                if v.l < L - 1:
                    return
                reach(pool, e_osum, v.no - ET * (L - 1) - AB + 1)
                pool.sem_inc(passed["pool"], 1)
                pool.indirect_dma_start(xe_in[v.r4], None, x,
                                        bass.IndirectOffsetOnAxis(gather_rows[v.r4][:, 1:2], 0)).then_inc(xe_landed[v.r4], 16)

            def rsqrt(v):
                pool.wait_ge(e_mv, v.no + 1)
                reach(pool, e_scaled, v.no - 1)
                pool.sem_inc(passed["pool"], 1)
                nc.gpsimd.tensor_scalar(veps[v.r2][:], mv[v.r2][:, 1:2], EPS, None, ALU.add).then_inc(e_veps, 1)
                pool.wait_ge(e_veps, v.no + 1)
                nc.gpsimd.tensor_tensor(rstd[v.r2][:], veps[v.r2][:], minus_half[:], ALU.pow).then_inc(e_rstd, 1)

            def add_shift(v):
                pool.wait_ge(e_scaled, v.no + 1)
                nc.gpsimd.tensor_tensor(y[v.r2][:], y[v.r2][:], shift[:, v.l, :], ALU.add).then_inc(e_shifted, 1)

            def out_rsqrt(v):
                if v.l < L - 1:
                    return
                n = v.no - ET * (L - 1)
                pool.wait_ge(e_omv, n + 1)
                reach(pool, e_o, n - 1)
                pool.sem_inc(passed["pool"], 1)
                nc.gpsimd.tensor_scalar(oveps[v.r2][:], omv[v.r2][:, 1:2], EPS, None, ALU.add).then_inc(e_oveps, 1)
                pool.wait_ge(e_oveps, n + 1)
                nc.gpsimd.tensor_tensor(orstd[v.r2][:], oveps[v.r2][:], minus_half[:], ALU.pow).then_inc(e_orstd, 1)
                pool.wait_ge(e_orstd, n + 1)
                pool.sem_inc(passed["pool"], 1)
                nc.gpsimd.tensor_scalar(omean[v.r2][:], omv[v.r2][:, 0:1], orstd[v.r2][:, 0:1], -1.0,
                                        ALU.mult, ALU.mult).then_inc(e_omean, 1)

            def scatter(v, ready, count):
                reach(pool, scattered[v.r4], 16 * v.use)
                pool.sem_inc(passed["pool"], 1)
                nc.gpsimd.tensor_copy(scatter_rows[v.r4][:], tile_rows(v, 2, 3)).then_inc(e_srows, 1)
                pool.wait_ge(e_srows, v.no + 1)
                pool.wait_ge(ready, count)
                pool.sem_inc(passed["pool"], 1)
                pool.indirect_dma_start(out if v.l == L - 1 else h_dram[v.l],
                                        bass.IndirectOffsetOnAxis(scatter_rows[v.r4][:, 0:1], 0), res[v.r4], None,
                                        bounds_check=N - 1, oob_is_err=False).then_inc(scattered[v.r4], 16)

            def scatter_h(v):
                if v.l < L - 1:
                    scatter(v, e_h, v.no + 1)

            def scatter_out(v):
                if v.l == L - 1:
                    scatter(v, e_o, v.no - ET * (L - 1) + 1)

            def slot(l, body, k):
                steps(l, body, k, (gather, 4), (gather_x, 1), (rsqrt, -1), (scatter_h, -3), (add_shift, -1),
                      (out_rsqrt, -3), (scatter_out, -4))

            all_tiles(pool, slot)
            for i in range(AB):
                pool.wait_ge(scattered[i], 16 * NB * L)

        def tile_rows(v, c0, c1):
            return rows_of[:, bass.ds(v.t, 1), c0:c1].rearrange("p a c -> p (a c)")

        def tensor_edges(pe):
            def turn(v):
                pe.wait_ge(self_landed[v.r4], 16 * (v.use + 1))
                reach(pe, e_low, v.no - 1)
                for k in range(KC):
                    mm = pe.transpose(ps_t[v.r2][:, k * P:(k + 1) * P], self_in[v.r4][:, k * P:(k + 1) * P], ident[:])
                mm.then_inc(e_turned, 1)

            def sum_messages(v):
                pe.wait_ge(e_same, v.no + 1)
                pe.wait_ge(e_mlow, v.no + 1)
                reach(pe, e_carry, v.no - 1)
                for k in range(KC):
                    pe.matmul(ps_s[v.r2][:, k * P:(k + 1) * P], m_hi[v.r2][:, k * P:(k + 1) * P], same[v.r2][:],
                              start=True, stop=False)
                    mm = pe.matmul(ps_s[v.r2][:, k * P:(k + 1) * P], m_lo[v.r2][:, k * P:(k + 1) * P], same[v.r2][:],
                                   start=False, stop=True)
                mm.then_inc(e_summed, 1)

            def product_self(v):
                reach(pe, e_z_sum, v.no - 1)
                pe.matmul(ps_z[v.r2][:], ones2[:], bias2[:, v.l, :], start=True, stop=False)
                pe.wait_ge(e_low, v.no + 1)
                mm3(pe, ps_z[v.r2], hT_hi[v.r2], hT_lo[v.r2], v.l, False, True).then_inc(e_z_ready, 1)

            def product_mean(v):
                pe.wait_ge(e_slow, v.no + 1)
                mm3(pe, ps_a[v.r2], sT_hi[v.r2], sT_lo[v.r2], L + v.l, True, True).then_inc(e_a_ready, 1)

            def slot(l, body, k):
                steps(l, body, k, (product_self, 0), (turn, 1), (sum_messages, 2), (product_mean, 0))

            all_tiles(pe, slot)

        def scalar_edges(act):
            def mean(v):
                act.wait_ge(e_a_ready, v.no + 1)
                reach(act, e_gained, v.no - 1)
                nc.scalar.activation(z_sb[v.r2], ps_a[v.r2][:], ACT.Identity,
                                     scale=rcount[:, bass.ds(v.t, 1)]).then_inc(e_mean, 1)

            def take_high(v):
                act.wait_ge(e_turned, v.no + 1)
                reach(act, e_z_ready, v.no - 1)
                nc.scalar.copy(flat(hT_hi[v.r2]), ps_t[v.r2][:]).then_inc(e_high, 1)

            def take_sum_high(v):
                act.wait_ge(e_carry, v.no + 1)
                reach(act, e_a_ready, v.no - 1)
                nc.scalar.copy(flat(sT_hi[v.r2]), sumT[v.r2]).then_inc(e_shigh, 1)

            def take_message_high(v):
                act.wait_ge(m_landed[v.r4], 16 * (v.use + 1))
                reach(act, e_summed, v.no - 1)
                nc.scalar.copy(m_hi[v.r2][:], m_in[v.r4]).then_inc(e_mhigh, 1)

            def part(v):
                act.wait_ge(e_shifted, v.no + 1)
                reach(act, e_h, v.no - 1)
                nc.scalar.activation(neg[v.r2][:], y[v.r2][:], ACT.Relu, scale=-1.0).then_inc(e_parted, 1)

            def scale(v):
                act.wait_ge(e_gained, v.no + 1)
                act.wait_ge(e_rstd, v.no + 1)
                nc.scalar.activation(y[v.r2][:], y[v.r2][:], ACT.Identity, scale=rstd[v.r2][:, 0:1]).then_inc(e_scaled, 1)

            def take_over(v):
                if isinstance(v.t, int) and v.t == 0:
                    return
                act.wait_ge(e_same, v.no + 1)
                act.wait_ge(e_carry, v.no)
                for k in range(KC):
                    ins = nc.scalar.activation(over[v.r2][:, k * P:(k + 1) * P], carried[v.r2], ACT.Identity,
                                               scale=sumT[1 - v.r2][:, (k + 1) * P - 1:(k + 1) * P])
                ins.then_inc(e_taken_over, 1)

            def out_norm(v):
                if v.l < L - 1:
                    return
                act.wait_ge(e_orstd, v.no - ET * (L - 1) + 1)
                act.wait_ge(e_omean, v.no - ET * (L - 1) + 1)
                nc.scalar.activation(res[v.r4], res[v.r4], ACT.Identity, scale=orstd[v.r2][:, 0:1],
                                     bias=omean[v.r2][:, 0:1]).then_inc(e_o, 1)

            def slot(l, body, k):
                steps(l, body, k, (mean, -1), (take_sum_high, 1), (take_message_high, 3), (take_over, 2), (part, -2),
                      (take_high, 1), (scale, -1), (out_norm, -3))

            all_tiles(act, slot)

        def vector_edges(dve):
            def add_products(v):
                dve.wait_ge(e_mean, v.no + 1)
                nc.vector.tensor_tensor(z_sb[v.r2], z_sb[v.r2], ps_z[v.r2][:], ALU.add).then_inc(e_z_sum, 1)

            def take_low(v):
                dve.wait_ge(e_high, v.no + 1)
                nc.vector.tensor_tensor(flat(hT_lo[v.r2]), ps_t[v.r2][:], flat(hT_hi[v.r2]).bitcast(F32),
                                        ALU.subtract).then_inc(e_low, 1)

            def carry(v):
                dve.wait_ge(e_summed, v.no + 1)
                reach(dve, e_slow, v.no - 1)
                if isinstance(v.t, int) and v.t == 0:
                    nc.vector.tensor_copy(sumT[v.r2], ps_s[v.r2][:]).then_inc(e_carry, 1)
                    return
                dve.wait_ge(e_taken_over, v.no - v.l)
                nc.vector.tensor_tensor(sumT[v.r2], over[v.r2], ps_s[v.r2][:], ALU.add).then_inc(e_carry, 1)

            def take_sum_low(v):
                dve.wait_ge(e_shigh, v.no + 1)
                nc.vector.tensor_tensor(flat(sT_lo[v.r2]), sumT[v.r2], flat(sT_hi[v.r2]).bitcast(F32),
                                        ALU.subtract).then_inc(e_slow, 1)

            def statistics(v):
                dve.wait_ge(e_z_sum, v.no + 1)
                nc.vector.bn_stats(stats[v.r2][:], z_sb[v.r2]).then_inc(e_stat, 1)

            def mean(v):
                dve.wait_ge(e_stat, v.no + 1)
                reach(dve, e_parted, v.no - 1)
                dve.sem_inc(passed["dve"], 1)
                nc.vector.bn_aggr(mv[v.r2][:], stats[v.r2][:]).then_inc(e_mv, 1)

            def normal(v):
                dve.wait_ge(e_mv, v.no + 1)
                nc.vector.scalar_tensor_tensor(y[v.r2][:], z_sb[v.r2], mv[v.r2][:, 0:1], gain[:, v.l, :],
                                               ALU.subtract, ALU.mult).then_inc(e_gained, 1)

            def compare(v):
                reach(dve, e_summed, v.no - 1)
                reach(dve, e_carry, v.no - 1)
                here = dst_row[:, bass.ds(v.t * P + 1, P)]
                if not (isinstance(v.t, int) and v.t == 0):
                    nc.vector.tensor_scalar(carried[v.r2], here, dst_row[:, bass.ds(v.t * P, 1)], None, ALU.is_equal)
                nc.vector.tensor_scalar(same[v.r2][:], here, dst_col[:, bass.ds(v.t, 1)], None,
                                        ALU.is_equal).then_inc(e_same, 1)

            def take_message_low(v):
                dve.wait_ge(e_mhigh, v.no + 1)
                nc.vector.tensor_tensor(m_lo[v.r2][:], m_in[v.r4], m_hi[v.r2][:].bitcast(F32),
                                        ALU.subtract).then_inc(e_mlow, 1)

            def prelu(v):
                dve.wait_ge(e_parted, v.no + 1)
                reach(dve, scattered[v.r4], 16 * v.use)
                nc.vector.scalar_tensor_tensor(res[v.r4], neg[v.r2][:], slope_less[:, 0:1], y[v.r2][:],
                                               ALU.mult, ALU.add).then_inc(e_h, 1)

            def out_sum(v):
                if v.l < L - 1:
                    return
                n = v.no - ET * (L - 1)
                dve.wait_ge(xe_landed[v.r4], 16 * (v.body + 1))
                dve.wait_ge(e_h, v.no + 1)
                nc.vector.tensor_tensor(res[v.r4], res[v.r4], xe_in[v.r4], ALU.add).then_inc(e_osum, 1)
                dve.wait_ge(e_osum, n + 1)
                nc.vector.bn_stats(ostats[v.r2][:], res[v.r4]).then_inc(e_ostat, 1)
                dve.wait_ge(e_ostat, n + 1)
                dve.sem_inc(passed["dve"], 1)
                nc.vector.bn_aggr(omv[v.r2][:], ostats[v.r2][:]).then_inc(e_omv, 1)

            def slot(l, body, k):
                steps(l, body, k, (carry, 1), (add_products, -1), (statistics, -1), (take_message_low, 3), (mean, -1),
                      (compare, 3), (normal, -1), (take_sum_low, 1), (prelu, -2), (take_low, 1), (out_sum, -2))

            all_tiles(dve, slot)

        with nc.Block() as block:
            block.gpsimd(gpsimd_edges)
            block.tensor(tensor_edges)
            block.scalar(scalar_edges)
            block.vector(vector_edges)


def flat(t):
    return t[:].rearrange("p k n -> p (k n)")


def kernel(**inputs):
    import concourse.bacc as bacc
    from concourse.bass_utils import run_bass_kernel_spmd

    nc = bacc.Bacc("TRN2", target_bir_lowering=False, num_devices=1)
    arrays = {}

    def given(name, array):
        array = np.ascontiguousarray(array)
        arrays[f"in_{name}"] = array
        return nc.dram_tensor(f"in_{name}", array.shape, mybir.dt.from_np(array.dtype), kind="ExternalInput").ap()

    N = inputs["x"].shape[0]
    E = inputs["src"].shape[0]
    ET = -(-E // P)
    per_layer = lambda name: [given(f"{name}{l}", inputs[f"L0_gnn_{name}{l}"]) for l in range(L)]
    ident = given("ident", np.eye(P, dtype=np.float32))
    edge_no = given("edge_no", np.arange(ET * P, dtype=np.float32).reshape(ET, P))
    row_select = given("row_select", np.eye(2, dtype=np.float32))
    dst_pad = given("dst_pad", np.array([-1] + [N] * (ET * P - E + 1), np.int32))
    src_pad = given("src_pad", np.zeros(P, np.int32))
    x = given("x", inputs["x"])
    out = nc.dram_tensor("out", x.shape, F32, kind="ExternalOutput").ap()
    build_program(nc, x, given("src", inputs["src"]), given("dst", inputs["dst"]),
                  per_layer("Wl"), per_layer("bl"), per_layer("Wr"), per_layer("g"), per_layer("b"),
                  given("a_prelu", inputs["L0_gnn_a_prelu"]), ident, edge_no, row_select, dst_pad, src_pad, out)
    result = run_bass_kernel_spmd(nc, [arrays], core_ids=[0])
    return result.results[0]["out"]
```

```python
from contextlib import ExitStack

import numpy as np

import concourse.bass as bass
from concourse import mybir

P = 128
ALU = mybir.AluOpType
ACT = mybir.ActivationFunctionType
F32 = mybir.dt.float32
F32R = mybir.dt.float32r
I32 = mybir.dt.int32
I16 = mybir.dt.int16

L = 3
TG = 4
UG = L * TG
EPS = 1e-5
FAR = 65536.0


def reach(eng, sem, count):
    if isinstance(count, int) and count <= 0:
        return
    eng.wait_ge(sem, count)


def build_program(nc, x, src, dst, Wl, bl, Wr, g, b, a_prelu, ident_in, edge_no_in, row_select_in,
                  dst_pad_in, src_pad_in, out):
    N, D = x.shape
    E = src.shape[0]
    KC = D // P
    GROUP = TG * P
    NG = N // GROUP
    REST = N - NG * GROUP
    ET = -(-E // P)
    EP = ET * P
    AB = 4
    assert N < 2 ** 15 and D == 512 and NG % 2 == 1 and NG >= 5 and 0 < REST <= P and ET % AB == 0 and ET >= 2 * AB
    NU = UG * NG
    UNITS = NU + L

    h_dram = [nc.dram_tensor(f"h{l + 1}_scratch", [N, D], F32).ap() for l in range(L - 1)]
    z_dram = nc.dram_tensor("z1_scratch", [N, D], F32).ap()
    dst_dram = nc.dram_tensor("dst_padded", [EP + 2], I32).ap()
    src_dram = nc.dram_tensor("src_padded", [EP], I32).ap()

    with ExitStack() as ctx:
        def sb(name, shape, dt=F32):
            return ctx.enter_context(nc.sbuf_tensor(name, shape, dt))

        def sem(name):
            return ctx.enter_context(nc.semaphore(name))

        WHOLE = L
        w_hi = [None if i == WHOLE else sb(f"w_hi{i}", [P, KC, D], F32R) for i in range(2 * L)]
        w_lo = [None if i == WHOLE else sb(f"w_lo{i}", [P, KC, D], F32R) for i in range(2 * L)]
        w_whole = sb("w_whole", [P, KC, D])
        bias2 = sb("bias2", [2, L, D], F32R)
        ones2 = sb("ones2", [2, P], F32R)
        gain = sb("gain", [P, L, D])
        shift = sb("shift", [P, L, D])
        slope = sb("slope", [P, 1])
        slope_less = sb("slope_less", [P, 1])
        minus_half = sb("minus_half", [P, 1])
        ident = sb("ident", [P, P])

        x_sb = [sb(f"x_sb{i}", [P, TG, D]) for i in range(2)]
        h_sb = [sb(f"h_sb{i}", [P, TG, D]) for i in range(L - 1)]
        o_sb = [sb(f"o_sb{i}", [P, TG, D]) for i in range(2)]
        hT_hi = [sb(f"hT_hi{i}", [P, KC, P], F32R) for i in range(2)]
        hT_lo = [sb(f"hT_lo{i}", [P, KC, P], F32R) for i in range(2)]
        y = [sb(f"y{i}", [P, D]) for i in range(2)]
        neg = [sb(f"neg{i}", [P, D]) for i in range(2)]
        stats = [sb(f"stats{i}", [P, 6]) for i in range(2)]
        mv = [sb(f"mv{i}", [P, 2]) for i in range(2)]
        veps = [sb(f"veps{i}", [P, 1]) for i in range(2)]
        rstd = [sb(f"rstd{i}", [P, 1]) for i in range(2)]
        ostats = [sb(f"ostats{i}", [P, 6]) for i in range(2)]
        omv = [sb(f"omv{i}", [P, 2]) for i in range(2)]
        oveps = [sb(f"oveps{i}", [P, 1]) for i in range(2)]
        omean = [sb(f"omean{i}", [P, 1]) for i in range(2)]
        orstd = [sb(f"orstd{i}", [P, 1]) for i in range(2)]

        dst_row = sb("dst_row", [P, EP + 1], I16)
        rows_of = sb("rows_of", [P, ET, 3], I32)
        rcount = sb("rcount", [P, ET])
        dst_col = sb("dst_col", [P, ET])
        gather_rows = [sb(f"gather_rows{i}", [P, 2], I32) for i in range(AB)]
        scatter_rows = [sb(f"scatter_rows{i}", [P, 1], I32) for i in range(AB)]

        dense_only = ExitStack()
        z_out = dense_only.enter_context(nc.sbuf_tensor("z_out", [P, TG, D], F32))
        rest_x, rest_h1, rest_h2, rest_out = [
            dense_only.enter_context(nc.sbuf_tensor(f"rest_{name}", [P, D], F32)) for name in ("x", "h1", "h2", "out")]

        ps = [ctx.enter_context(nc.psum_tensor(f"ps{i}", [P, D], F32)) for i in range(8)]
        ps_t, ps_z, ps_a, ps_s = ps[0:2], ps[2:4], ps[4:6], ps[6:8]
        ZB = 4
        z_banks = ps[2:2 + ZB]

        passed = {e: sem(f"passed_{e}") for e in ("dve", "pool")}

        stage = [o_sb[0], o_sb[1], h_sb[0], h_sb[1]]
        WORDER = [("r", l) for l in range(L)] + [("l", l) for l in range(L)]
        DIAGONAL = [("r", l) for l in range(1, L)]
        x_in = [sem(f"x_in{i}") for i in range(2)]

        def group_view(dram, first_row):
            return dram[bass.ds(first_row, GROUP), :].rearrange("(p j) d -> p j d", j=TG)

        with ExitStack() as sctx:
            def ssb(name, shape, dt=F32):
                return sctx.enter_context(nc.sbuf_tensor(name, shape, dt))

            def ssem(name):
                return sctx.enter_context(nc.semaphore(name))

            room = x_sb[1][:].rearrange("p j d -> p (j d)")
            lists = room[0:ET, 0:4 * P].bitcast(I32).rearrange("t (c p) -> t c p", c=4)
            listf = room[0:ET, 4 * P:8 * P].rearrange("t (c p) -> t c p", c=4)
            cols = room[0:ET, 8 * P:13 * P].rearrange("t (c p) -> t c p", c=5)
            edge_no = room[0:ET, 13 * P:14 * P]
            first = room[0:ET, 14 * P:15 * P]
            run = room[0:ET, 15 * P:16 * P]
            bias_raw = [t[0:2, :] for t in (rest_h1, rest_h2, rest_out)]
            last_run = y[0][0:ET, 0:1]
            before = y[0][0:ET, 1:2]
            row_select = y[0][0:2, 2:3]
            runs_before = y[0][0:1, 4:5 + ET]
            zero_row = y[0][0:1, 2 * P:2 * P + ET]
            w_banks = ps[0:5]
            ps_runs, ps_before, ps_cols = ps[5:8]

            w_in = [ssem(f"w_in{i}") for i in range(4)]
            ident_in_sem = ssem("ident_in_sem")
            const_in = ssem("const_in")
            lists_copied = ssem("lists_copied")
            lists_in = ssem("lists_in")
            row_in = ssem("row_in")
            w_turned = ssem("w_turned")
            w_diag = ssem("w_diag")
            w_high = ssem("w_high")
            w_low = ssem("w_low")
            w_copied = ssem("w_copied")
            prep = ssem("prep")
            slope_in = ssem("slope_in")
            affine_in = ssem("affine_in")
            small_turned = ssem("small_turned")
            run_done = ssem("run_done")
            bias_high = ssem("bias_high")
            ready = ssem("ready")

            def split_chunks(n):
                return n if n < KC * WHOLE else n - KC

            with nc.Block() as block:
                @block.sync
                def _(sp):
                    def load_weight(i):
                        side, l = WORDER[i]
                        w = (Wr if side == "r" else Wl)[l]
                        if i >= 4:
                            sp.wait_ge(w_turned, KC * (i - 3))
                        sp.dma_start(stage[i % 4][:], w.rearrange("(c p) k -> p c k", p=P)).then_inc(w_in[i % 4], 16)

                    sp.dma_start(ident[:], ident_in).then_inc(ident_in_sem, 16)
                    sp.dma_start(dst_dram[1:E + 1], dst).then_inc(lists_copied, 16)
                    sp.dma_start(dst_dram[0:1], dst_pad_in[0:1]).then_inc(lists_copied, 16)
                    sp.dma_start(dst_dram[E + 1:EP + 2], dst_pad_in[1:EP - E + 2]).then_inc(lists_copied, 16)
                    sp.dma_start(src_dram[0:E], src).then_inc(lists_copied, 16)
                    if EP > E:
                        sp.dma_start(src_dram[E:EP], src_pad_in[0:EP - E]).then_inc(lists_copied, 16)
                    load_weight(0)
                    load_weight(1)
                    sp.wait_ge(lists_copied, 16 * (4 + (EP > E)))
                    tiled = lambda v: v.rearrange("(t p) -> t p", p=P)
                    sp.dma_start(lists[:, 0, :], tiled(dst_dram[1:EP + 1])).then_inc(lists_in, 16)
                    sp.dma_start(lists[:, 1, :], tiled(dst_dram[2:EP + 2])).then_inc(lists_in, 16)
                    sp.dma_start(lists[:, 2, :], tiled(dst_dram[0:EP])).then_inc(lists_in, 16)
                    sp.dma_start(lists[:, 3, :], tiled(src_dram)).then_inc(lists_in, 16)
                    sp.dma_start(edge_no, edge_no_in).then_inc(lists_in, 16)
                    load_weight(2)
                    load_weight(3)
                    sp.dma_start(row_select, row_select_in).then_inc(const_in, 16)
                    for l in range(L):
                        sp.dma_start(bias_raw[l], bl[l].rearrange("(a d) -> a d", a=1).to_broadcast([2, D])).then_inc(const_in, 16)
                    for i in range(4, 2 * L):
                        load_weight(i)
                    sp.dma_start(slope[:], a_prelu.rearrange("(a c) -> a c", a=1).to_broadcast([P, 1])).then_inc(slope_in, 16)
                    sp.dma_start(x_sb[0][:], group_view(x, 0)).then_inc(x_in[0], 16)
                    for l in range(L):
                        sp.dma_start(gain[:, l, :], g[l].rearrange("(a d) -> a d", a=1).to_broadcast([P, D])).then_inc(affine_in, 16)
                        sp.dma_start(shift[:, l, :], b[l].rearrange("(a d) -> a d", a=1).to_broadcast([P, D])).then_inc(affine_in, 16)
                    sp.wait_ge(affine_in, 2 * 16 * L)

                @block.tensor
                def _(pe):
                    def turn_weight(i):
                        pe.wait_ge(w_in[i % 4], 16 * (i // 4 + 1))
                        if WORDER[i] in DIAGONAL:
                            pe.wait_ge(w_diag, DIAGONAL.index(WORDER[i]) + 1)
                        for k in range(KC):
                            n = KC * i + k
                            last = n - len(w_banks)
                            if last >= 0 and last // KC == WHOLE:
                                pe.wait_ge(w_copied, last - KC * WHOLE + 1)
                            elif last >= 0:
                                pe.wait_ge(w_low, split_chunks(last) + 1)
                            for c in range(KC):
                                mm = pe.transpose(w_banks[n % len(w_banks)][:, c * P:(c + 1) * P],
                                                  stage[i % 4][:, c, k * P:(k + 1) * P], ident[:])
                            mm.then_inc(w_turned, 1)

                    pe.wait_ge(ident_in_sem, 16)
                    for i in range(3):
                        turn_weight(i)
                    pe.wait_ge(prep, 4)
                    pe.transpose(ps_runs[0:1, 0:ET], last_run, ident[0:ET, 0:ET]).then_inc(small_turned, 1)
                    turn_weight(3)
                    pe.wait_ge(prep, 5)
                    pe.transpose(ps_before[0:ET, 0:1], runs_before[0:1, 0:ET], ident[0:1, 0:1]).then_inc(small_turned, 1)
                    turn_weight(4)
                    pe.wait_ge(prep, 12)
                    for c in range(5):
                        mm = pe.transpose(ps_cols[:, c * ET:(c + 1) * ET], cols[:, c, :], ident[0:ET, 0:ET])
                    mm.then_inc(small_turned, 1)
                    turn_weight(5)

                @block.scalar
                def _(act):
                    for i in range(2 * L):
                        if i == 4:
                            act.wait_ge(const_in, 16 * (1 + L))
                            for l in range(L):
                                nc.scalar.copy(bias2[:, l, :], bias_raw[l]).then_inc(bias_high, 1)
                        for k in range(KC):
                            n = KC * i + k
                            act.wait_ge(w_turned, n + 1)
                            if i == WHOLE:
                                nc.scalar.copy(w_whole[:, k, :], w_banks[n % len(w_banks)][:]).then_inc(w_copied, 1)
                            else:
                                nc.scalar.copy(w_hi[i][:, k, :], w_banks[n % len(w_banks)][:]).then_inc(w_high, 1)

                @block.gpsimd
                def _(pool):
                    pool.wait_ge(lists_copied, 16 * (4 + (EP > E)))
                    pool.dma_start(dst_row[:], dst_dram[0:EP + 1].rearrange("(a d) -> a d", a=1)
                                   .to_broadcast([P, EP + 1])).then_inc(row_in, 16)
                    pool.wait_ge(ident_in_sem, 16)
                    for i, which in enumerate(WORDER):
                        if which in DIAGONAL:
                            pool.wait_ge(w_in[i % 4], 16 * (i // 4 + 1))
                            for c in range(KC):
                                diag = stage[i % 4][:, c, c * P:(c + 1) * P]
                                ins = nc.gpsimd.tensor_tensor(diag, diag, ident[:], ALU.add)
                            ins.then_inc(w_diag, 1)
                    pool.wait_ge(row_in, 16)

                @block.vector
                def _(dve):
                    def split_low(i):
                        for k in range(KC):
                            n = KC * i + k
                            dve.wait_ge(w_high, split_chunks(n) + 1)
                            nc.vector.tensor_tensor(w_lo[i][:, k, :], w_banks[n % len(w_banks)][:],
                                                    w_hi[i][:, k, :].bitcast(F32), ALU.subtract).then_inc(w_low, 1)

                    step = [0]

                    def then(ins):
                        step[0] += 1
                        ins.then_inc(prep, 1)
                        dve.wait_ge(prep, step[0])

                    nc.vector.memset(ones2[:].bitcast(F32), 1.0)
                    nc.vector.memset(minus_half[:], -0.5)
                    nc.vector.memset(runs_before[:, 0:1], 0.0)
                    nc.vector.memset(rest_x[:], 0.0)
                    nc.vector.memset(zero_row, 0.0).then_inc(ready, 1)
                    split_low(0)
                    split_low(1)
                    dve.wait_ge(ready, 1)
                    dve.wait_ge(lists_in, 16 * 5)
                    then(nc.vector.tensor_copy(listf, lists))
                    then(nc.vector.tensor_tensor(first, listf[:, 0, :], listf[:, 2, :], ALU.not_equal))
                    then(nc.vector.tensor_tensor(first, first, edge_no, ALU.mult))
                    nc.vector.tensor_tensor_scan(run, first, first, 0.0, ALU.max, ALU.max).then_inc(run_done, 1)
                    dve.wait_ge(run_done, 1)
                    then(nc.vector.tensor_copy(last_run, run[:, P - 1:P]))
                    split_low(2)
                    dve.wait_ge(small_turned, 1)
                    then(nc.vector.tensor_tensor_scan(runs_before[:, 1:ET + 1], ps_runs[0:1, 0:ET], zero_row,
                                                      0.0, ALU.max, ALU.max))
                    dve.wait_ge(small_turned, 2)
                    then(nc.vector.tensor_copy(before, ps_before[0:ET, 0:1]))
                    then(nc.vector.tensor_scalar(run, run, before[:, 0:1], -1.0, ALU.max, ALU.mult))
                    then(nc.vector.scalar_tensor_tensor(first, edge_no, 1.0, run, ALU.add, ALU.add))
                    then(nc.vector.reciprocal(cols[:, 3, :], first))
                    nc.vector.tensor_copy(cols[:, 0, :], listf[:, 3, :])
                    nc.vector.tensor_copy(cols[:, 4, :], listf[:, 0, :])
                    then(nc.vector.tensor_scalar(cols[:, 1, :], listf[:, 0, :], float(N - 1), None, ALU.min))
                    then(nc.vector.tensor_tensor(run, listf[:, 0, :], listf[:, 1, :], ALU.is_equal))
                    then(nc.vector.scalar_tensor_tensor(cols[:, 2, :], run, FAR, listf[:, 0, :], ALU.mult, ALU.add))
                    split_low(4)
                    split_low(5)
                    dve.wait_ge(bias_high, L)
                    for l in range(L):
                        nc.vector.scalar_tensor_tensor(bias2[:, l, :], bias2[:, l, :].bitcast(F32), row_select,
                                                       bias_raw[l], ALU.mult, ALU.add)
                    dve.wait_ge(small_turned, 3)
                    nc.vector.tensor_copy(rows_of[:].rearrange("p t c -> p c t"),
                                          ps_cols[:, 0:3 * ET].rearrange("p (c t) -> p c t", c=3))
                    nc.vector.tensor_copy(rcount[:], ps_cols[:, 3 * ET:4 * ET])
                    nc.vector.tensor_copy(dst_col[:], ps_cols[:, 4 * ET:5 * ET])
                    dve.wait_ge(slope_in, 16)
                    nc.vector.tensor_scalar(slope_less[:], slope[:], -1.0, 1.0, ALU.mult, ALU.add)

        rest_in = sem("rest_in")
        turned = sem("turned")
        high = sem("high")
        low = sem("low")
        z_ready = sem("z_ready")
        stat_done = sem("stat_done")
        mv_done = sem("mv_done")
        gained = sem("gained")
        veps_done = sem("veps_done")
        rstd_done = sem("rstd_done")
        scaled = sem("scaled")
        shifted = sem("shifted")
        parted = sem("parted")
        z_copied = sem("z_copied")
        z_stored = sem("z_stored")
        h_done = sem("h_done")
        summed = sem("summed")
        ostat_done = sem("ostat_done")
        omv_done = sem("omv_done")
        oveps_done = sem("oveps_done")
        orstd_done = sem("orstd_done")
        omean_done = sem("omean_done")
        o_done = sem("o_done")
        h_stored = [sem(f"h_stored{i}") for i in range(L - 1)]
        o_stored = [sem(f"o_stored{i}") for i in range(2)]

        rest_h = [rest_h1, rest_h2]
        LAST_UNITS = L * (TG + 1)

        class Unit:

            def __init__(self, half, par, k):
                while k < 0:
                    half, par, k = (half, 0, k + UG) if par else (half - 1, 1, k + UG)
                while k >= UG and not self.is_last(half, par):
                    half, par, k = (half + 1, 0, k - UG) if par else (half, 1, k - UG)
                self.half, self.par, self.k = half, par, k
                self.tiles = TG + 1 if self.is_last(half, par) else TG
                self.l, self.j = k // self.tiles, k % self.tiles
                self.group = 2 * half + par
                self.base = 2 * UG * half + UG * par
                self.no = self.base + k
                self.ring = k % 2
                self.bank = k % ZB
                self.firsts = 2 * TG * half + TG * par + self.j + 1

            @staticmethod
            def is_last(half, par):
                return isinstance(half, int) and 2 * half + par == NG - 1

            def exists(self):
                return not isinstance(self.no, int) or 0 <= self.no < UNITS

            def source(self):
                if self.j == TG:
                    return rest_x[:] if self.l == 0 else rest_h[self.l - 1][:]
                return x_sb[self.par][:, self.j, :] if self.l == 0 else h_sb[self.l - 1][:, self.j, :]

            def target(self):
                if self.j == TG:
                    return rest_h[self.l][:] if self.l < L - 1 else rest_out[:]
                return h_sb[self.l][:, self.j, :] if self.l < L - 1 else o_sb[self.par][:, self.j, :]

        class Output:

            def __init__(self, half, par, j):
                self.j, self.ring = j, j % 2
                self.no = 2 * TG * half + TG * par + j
                last = Unit.is_last(half, par)
                self.units = 2 * UG * half + UG * par + (L - 1) * (TG + last) + j + 1
                self.o = rest_out[:] if j == TG else o_sb[par][:, j, :]
                self.x = rest_x[:] if j == TG else x_sb[par][:, j, :]

        def slots(half, par):
            return LAST_UNITS + 5 if Unit.is_last(half, par) else UG

        def output_steps(half, par, k, sum0=None, sum1=None, whole_sum=None, stats_=None, root=None, norm=None):
            prev = Unit(half, par, -UG)
            if whole_sum and Unit.is_last(half, par):
                j = k - (L - 1) * (TG + 1) - 2
                if 0 <= j <= TG:
                    whole_sum(Output(half, par, j))
            for step, back in ((norm, 3), (root, 2), (stats_, 2), (sum1, 1), (sum0, 0)):
                if not step:
                    continue
                first = k - back + 1
                if prev.exists() and first % 3 == 0 and k >= 0 and 0 <= first // 3 < TG:
                    step(Output(prev.half, prev.par, first // 3))
                if not Unit.is_last(half, par):
                    if k - back + 1 == UG:
                        step(Output(half, par, 0))
                elif back > 1:
                    j = k - back - (L - 1) * (TG + 1) - 1
                    if 0 <= j <= TG:
                        step(Output(half, par, j))

        def all_groups(eng, group):
            group(0, 0)
            with eng.Fori(0, (NG - 3) // 2) as i:
                group(i, 1)
                group(i + 1, 0)
            group((NG - 3) // 2, 1)
            group((NG - 1) // 2, 0)

        def sync_dense(sp):
            def load_x(half, par, group):
                sp.dma_start(x_sb[par][:], group_view(x, GROUP * group)).then_inc(x_in[par], 16)

            def group(half, par):
                u = Unit(half, par, 0)
                sp.wait_ge(z_copied, Unit(half, par, TG - 1).firsts)
                sp.dma_start(group_view(z_dram, GROUP * u.group), z_out[:]).then_inc(z_stored, 16)
                sp.wait_ge(h_done, u.no + TG)
                sp.dma_start(group_view(h_dram[0], GROUP * u.group), h_sb[0][:]).then_inc(h_stored[0], 16)
                if not (isinstance(half, int) and u.group == 0):
                    prev = Unit(half, par, -UG)
                    sp.wait_ge(summed, TG * u.group)
                    if not (isinstance(half, int) and u.group == NG - 1):
                        load_x(prev.half, prev.par, u.group + 1)
                    sp.wait_ge(o_done, TG * u.group)
                    sp.dma_start(group_view(out, GROUP * prev.group), o_sb[prev.par][:]).then_inc(o_stored[prev.par], 16)
                sp.wait_ge(h_done, u.no + u.tiles + TG)
                sp.dma_start(group_view(h_dram[1], GROUP * u.group), h_sb[1][:]).then_inc(h_stored[1], 16)

            load_x(0, 1, 1)
            sp.dma_start(rest_x[0:REST], x[NG * GROUP:N, :]).then_inc(rest_in, 16)
            all_groups(sp, group)
            sp.wait_ge(z_copied, TG * NG + 1)
            sp.dma_start(z_dram[NG * GROUP:N, :], rest_out[0:REST]).then_inc(z_stored, 16)
            for l in range(L - 1):
                sp.wait_ge(h_done, NU - UG + (TG + 1) * (l + 1))
                sp.dma_start(h_dram[l][NG * GROUP:N, :], rest_h[l][0:REST]).then_inc(h_stored[l], 16)
            sp.wait_ge(o_done, TG * NG)
            sp.dma_start(group_view(out, GROUP * (NG - 1)), o_sb[(NG - 1) % 2][:]).then_inc(o_stored[(NG - 1) % 2], 16)
            sp.wait_ge(o_done, TG * NG + 1)
            sp.dma_start(out[NG * GROUP:N, :], rest_out[0:REST]).then_inc(o_stored[NG % 2], 16)
            sp.wait_ge(z_stored, 16 * (NG + 1))
            for l in range(L - 1):
                sp.wait_ge(h_stored[l], 16 * (NG + 1))
            sp.wait_ge(o_stored[0], 16 * (-(-NG // 2)))
            sp.wait_ge(o_stored[1], 16 * (NG // 2 + 1))

        def mm3(pe, acc, aT_hi, aT_lo, w, start, stop, chunks=range(KC)):
            for k in chunks:
                for a, ww in ((aT_hi, w_hi[w]), (aT_hi, w_lo[w]), (aT_lo, w_hi[w])):
                    mm = pe.matmul(acc[:], a[:, k, :], ww[:, k, :], start=start, stop=stop and k == KC - 1 and a is aT_lo)
                    start = False
            return mm

        def tensor_dense(pe):
            def turn(u):
                if u.j == TG and u.l == 0:
                    pe.wait_ge(rest_in, 16)
                elif u.l == 0:
                    pe.wait_ge(x_in[u.par], 16 * (u.half + 1))
                else:
                    pe.wait_ge(h_done, u.no - u.tiles + 1)
                reach(pe, low, u.no - 1)
                for k in range(KC):
                    mm = pe.transpose(ps_t[u.ring][:, k * P:(k + 1) * P], u.source()[:, k * P:(k + 1) * P], ident[:])
                mm.then_inc(turned, 1)

            def begin_product(u):
                before = Unit(u.half, u.par, u.k - ZB)
                reach(pe, gained, u.no - ZB + 1)
                if before.exists() and before.l == 0:
                    pe.wait_ge(z_copied, before.firsts)
                pe.matmul(z_banks[u.bank][:], ones2[:], bias2[:, u.l, :], start=True, stop=False)
                pe.wait_ge(low, u.no + 1)
                mm3(pe, z_banks[u.bank], hT_hi[u.ring], hT_lo[u.ring], u.l, False, True, range(1))

            def end_product(u):
                mm3(pe, z_banks[u.bank], hT_hi[u.ring], hT_lo[u.ring], u.l, False, True, range(1, KC)).then_inc(z_ready, 1)

            def group(half, par):
                for k in range(slots(half, par)):
                    for stage_, ahead in ((begin_product, 0), (turn, 1), (end_product, 0)):
                        u = Unit(half, par, k + ahead)
                        if u.exists():
                            stage_(u)

            turn(Unit(0, 0, 0))
            all_groups(pe, group)

        def scalar_dense(act):
            def take_high(u):
                act.wait_ge(turned, u.no + 1)
                reach(act, z_ready, u.no - 1)
                nc.scalar.copy(flat(hT_hi[u.ring]), ps_t[u.ring][:]).then_inc(high, 1)

            def scale(u):
                act.wait_ge(gained, u.no + 1)
                act.wait_ge(rstd_done, u.no + 1)
                nc.scalar.activation(y[u.ring][:], y[u.ring][:], ACT.Identity, scale=rstd[u.ring][:, 0:1]).then_inc(scaled, 1)

            def copy_first_product(u):
                if u.l > 0:
                    return
                act.wait_ge(gained, u.no + 1)
                if u.j < TG:
                    reach(act, z_stored, 16 * u.group)
                nc.scalar.copy(z_out[:, u.j, :] if u.j < TG else rest_out[:], z_banks[u.bank][:]).then_inc(z_copied, 1)

            def part(u):
                act.wait_ge(shifted, u.no + 1)
                reach(act, h_done, u.no - 1)
                nc.scalar.activation(neg[u.ring][:], y[u.ring][:], ACT.Relu, scale=-1.0).then_inc(parted, 1)

            def out_norm(t):
                act.wait_ge(orstd_done, t.no + 1)
                act.wait_ge(omean_done, t.no + 1)
                nc.scalar.activation(t.o, t.o, ACT.Identity, scale=orstd[t.ring][:, 0:1],
                                     bias=omean[t.ring][:, 0:1]).then_inc(o_done, 1)

            def group(half, par):
                for k in range(slots(half, par)):
                    for stage_, ahead in ((take_high, 1), (part, -2), (scale, -1), (copy_first_product, -1)):
                        u = Unit(half, par, k + ahead)
                        if u.exists():
                            stage_(u)
                    output_steps(half, par, k, norm=out_norm)

            take_high(Unit(0, 0, 0))
            all_groups(act, group)

        def gpsimd_dense(pool):
            def rsqrt(u):
                pool.wait_ge(mv_done, u.no + 1)
                reach(pool, scaled, u.no - 1)
                pool.sem_inc(passed["pool"], 1)
                nc.gpsimd.tensor_scalar(veps[u.ring][:], mv[u.ring][:, 1:2], EPS, None, ALU.add).then_inc(veps_done, 1)
                pool.wait_ge(veps_done, u.no + 1)
                nc.gpsimd.tensor_tensor(rstd[u.ring][:], veps[u.ring][:], minus_half[:], ALU.pow).then_inc(rstd_done, 1)

            def add_shift(u):
                pool.wait_ge(scaled, u.no + 1)
                nc.gpsimd.tensor_tensor(y[u.ring][:], y[u.ring][:], shift[:, u.l, :], ALU.add).then_inc(shifted, 1)

            def out_sum_left(t):
                pool.wait_ge(h_done, t.units)
                nc.gpsimd.tensor_tensor(t.o[:, 0:D // 2], t.o[:, 0:D // 2], t.x[:, 0:D // 2], ALU.add)

            def out_sum_right(t):
                nc.gpsimd.tensor_tensor(t.o[:, D // 2:D], t.o[:, D // 2:D], t.x[:, D // 2:D], ALU.add).then_inc(summed, 1)

            def out_rsqrt(t):
                pool.wait_ge(omv_done, t.no + 1)
                if isinstance(t.no, int):
                    reach(pool, o_done, t.no - 1)
                pool.sem_inc(passed["pool"], 1)
                nc.gpsimd.tensor_scalar(oveps[t.ring][:], omv[t.ring][:, 1:2], EPS, None, ALU.add).then_inc(oveps_done, 1)
                pool.wait_ge(oveps_done, t.no + 1)
                nc.gpsimd.tensor_tensor(orstd[t.ring][:], oveps[t.ring][:], minus_half[:], ALU.pow).then_inc(orstd_done, 1)
                pool.wait_ge(orstd_done, t.no + 1)
                pool.sem_inc(passed["pool"], 1)
                nc.gpsimd.tensor_scalar(omean[t.ring][:], omv[t.ring][:, 0:1], orstd[t.ring][:, 0:1], -1.0,
                                        ALU.mult, ALU.mult).then_inc(omean_done, 1)

            def group(half, par):
                for k in range(slots(half, par)):
                    u = Unit(half, par, k - 1)
                    if u.exists():
                        rsqrt(u)
                    output_steps(half, par, k, sum0=out_sum_left, sum1=out_sum_right, root=out_rsqrt)
                    if u.exists():
                        add_shift(u)

            all_groups(pool, group)

        def vector_dense(dve):
            def take_low(u):
                dve.wait_ge(high, u.no + 1)
                reach(dve, z_ready, u.no - 1)
                nc.vector.tensor_tensor(flat(hT_lo[u.ring]), ps_t[u.ring][:],
                                        flat(hT_hi[u.ring]).bitcast(F32),
                                        ALU.subtract).then_inc(low, 1)

            def statistics(u):
                dve.wait_ge(z_ready, u.no + 1)
                nc.vector.bn_stats(stats[u.ring][:], z_banks[u.bank][:]).then_inc(stat_done, 1)

            def mean(u):
                dve.wait_ge(stat_done, u.no + 1)
                reach(dve, parted, u.no - 1)
                dve.sem_inc(passed["dve"], 1)
                nc.vector.bn_aggr(mv[u.ring][:], stats[u.ring][:]).then_inc(mv_done, 1)

            def normal(u):
                dve.wait_ge(mv_done, u.no + 1)
                nc.vector.scalar_tensor_tensor(y[u.ring][:], z_banks[u.bank][:], mv[u.ring][:, 0:1], gain[:, u.l, :],
                                               ALU.subtract, ALU.mult).then_inc(gained, 1)

            def prelu(u):
                dve.wait_ge(parted, u.no + 1)
                if u.j == TG:
                    if u.l == L - 1:
                        dve.wait_ge(z_stored, 16 * (NG + 1))
                elif u.l < L - 1:
                    reach(dve, turned, u.base + (TG * (u.l + 1) + u.j + 1 - UG))
                    reach(dve, h_stored[u.l], 16 * u.group)
                else:
                    reach(dve, o_stored[u.par], 16 * u.half)
                nc.vector.scalar_tensor_tensor(u.target(), neg[u.ring][:], slope_less[:, 0:1], y[u.ring][:],
                                               ALU.mult, ALU.add).then_inc(h_done, 1)

            def out_sum(t):
                dve.wait_ge(h_done, t.units)
                nc.vector.tensor_tensor(t.o, t.o, t.x, ALU.add).then_inc(summed, 1)

            def out_statistics(t):
                dve.wait_ge(summed, t.no + 1)
                nc.vector.bn_stats(ostats[t.ring][:], t.o).then_inc(ostat_done, 1)

            def out_mean(t):
                dve.wait_ge(ostat_done, t.no + 1)
                dve.sem_inc(passed["dve"], 1)
                nc.vector.bn_aggr(omv[t.ring][:], ostats[t.ring][:]).then_inc(omv_done, 1)

            def group(half, par):
                for k in range(slots(half, par)):
                    u = Unit(half, par, k - 1)
                    if u.exists():
                        statistics(u)
                    output_steps(half, par, k, stats_=out_statistics)
                    if u.exists():
                        mean(u)
                    output_steps(half, par, k, stats_=out_mean)
                    if u.exists():
                        normal(u)
                    for stage_, ahead in ((take_low, 1), (prelu, -2)):
                        u = Unit(half, par, k + ahead)
                        if u.exists():
                            stage_(u)
                    output_steps(half, par, k, whole_sum=out_sum)

            take_low(Unit(0, 0, 0))
            all_groups(dve, group)

        with nc.Block() as block:
            block.sync(sync_dense)
            block.tensor(tensor_dense)
            block.scalar(scalar_dense)
            block.gpsimd(gpsimd_dense)
            block.vector(vector_dense)

        dense_only.close()
        same = [sb(f"same{i}", [P, P]) for i in range(2)]
        sT_hi = [sb(f"sT_hi{i}", [P, KC, P], F32R) for i in range(2)]
        sT_lo = [sb(f"sT_lo{i}", [P, KC, P], F32R) for i in range(2)]
        m_in = [h_sb[0][:, i, :] for i in range(AB)]
        self_in = [h_sb[1][:, i, :] for i in range(AB)]
        xe_in = [x_sb[0][:, i, :] for i in range(AB)]
        res = [o_sb[0][:, i, :] for i in range(AB)]
        sumT = [o_sb[1][:, i, :] for i in range(2)]
        z_sb = [o_sb[1][:, 2 + i, :] for i in range(2)]
        carried = [x_sb[1][:, i, 0:P] for i in range(2)]
        over = [x_sb[1][:, 2 + i, :] for i in range(2)]
        NB = ET // AB

        m_landed = [sem(f"m_landed{i}") for i in range(AB)]
        self_landed = [sem(f"self_landed{i}") for i in range(AB)]
        xe_landed = [sem(f"xe_landed{i}") for i in range(AB)]
        scattered = [sem(f"scattered{i}") for i in range(AB)]
        e_rows = sem("e_rows")
        e_srows = sem("e_srows")
        e_turned = sem("e_turned")
        e_summed = sem("e_summed")
        e_z_ready = sem("e_z_ready")
        e_a_ready = sem("e_a_ready")
        e_high = sem("e_high")
        e_shigh = sem("e_shigh")
        e_mean = sem("e_mean")
        e_scaled = sem("e_scaled")
        e_parted = sem("e_parted")
        e_z_sum = sem("e_z_sum")
        e_low = sem("e_low")
        e_carry = sem("e_carry")
        e_slow = sem("e_slow")
        e_same = sem("e_same")
        e_stat = sem("e_stat")
        e_mv = sem("e_mv")
        e_gained = sem("e_gained")
        e_h = sem("e_h")
        e_osum = sem("e_osum")
        e_ostat = sem("e_ostat")
        e_omv = sem("e_omv")
        e_o = sem("e_o")
        e_veps = sem("e_veps")
        e_rstd = sem("e_rstd")
        e_shifted = sem("e_shifted")
        e_oveps = sem("e_oveps")
        e_orstd = sem("e_orstd")
        e_omean = sem("e_omean")
        e_taken_over = sem("e_taken_over")

        class Edges:

            def __init__(self, l, body, k):
                body, k = body + k // AB, k % AB
                self.l, self.body = l, body
                self.t = AB * body + k
                self.no = ET * l + self.t
                self.r4, self.r2 = k, k % 2
                self.use = NB * l + body
                self.turns = self.no - ET

            def exists(self):
                return not isinstance(self.t, int) or 0 <= self.t < ET

        def all_tiles(eng, slot):
            for l in range(L):
                for k in range(-3, 2 * AB):
                    slot(l, 0, k)
                if NB > 3:
                    with eng.Fori(2, NB - 1) as body:
                        for k in range(AB):
                            slot(l, body, k)
                if NB > 2:
                    for k in range(AB):
                        slot(l, NB - 1, k)
                for k in range(6):
                    slot(l, NB, k)

        def steps(l, body, k, *todo):
            for step_, ahead in todo:
                v = Edges(l, body, k + ahead)
                if v.exists():
                    step_(v)

        STORED_PRODUCT = (0,)
        WHOLE_PRODUCT = (0,)
        VECTOR_SHIFTS = (0, L - 1)

        def h_in(l):
            return x if l == 0 else h_dram[l - 1]

        def gpsimd_edges(pool):
            def gather(v):
                reach(pool, m_landed[v.r4], 16 * v.use)
                reach(pool, self_landed[v.r4], 16 * v.use)
                if v.l == L - 1:
                    reach(pool, xe_landed[v.r4], 16 * v.body)
                pool.sem_inc(passed["pool"], 1)
                nc.gpsimd.tensor_copy(gather_rows[v.r4][:], tile_rows(v, 0, 2)).then_inc(e_rows, 1)
                pool.wait_ge(e_rows, v.no + 1)
                if isinstance(v.t, int) and v.t == 0 and v.l > 0:
                    for i in range(AB):
                        pool.wait_ge(scattered[i], 16 * NB * v.l)
                reach(pool, e_summed, v.no - AB + 1)
                pool.sem_inc(passed["pool"], 1)
                pool.indirect_dma_start(m_in[v.r4], None, h_in(v.l),
                                        bass.IndirectOffsetOnAxis(gather_rows[v.r4][:, 0:1], 0)).then_inc(m_landed[v.r4], 16)

            def gather_self(v):
                if v.l == 0 or (v.l == 1 and isinstance(v.t, int) and v.t < AB):
                    reach(pool, e_z_sum, v.no - AB + 1)
                else:
                    reach(pool, e_turned, v.turns - AB + 1)
                pool.sem_inc(passed["pool"], 1)
                pool.indirect_dma_start(self_in[v.r4], None, z_dram if v.l in STORED_PRODUCT else h_in(v.l),
                                        bass.IndirectOffsetOnAxis(gather_rows[v.r4][:, 1:2], 0)).then_inc(self_landed[v.r4], 16)

            def gather_x(v):
                if v.l < L - 1:
                    return
                reach(pool, e_osum, v.no - ET * (L - 1) - AB + 1)
                pool.sem_inc(passed["pool"], 1)
                pool.indirect_dma_start(xe_in[v.r4], None, x,
                                        bass.IndirectOffsetOnAxis(gather_rows[v.r4][:, 1:2], 0)).then_inc(xe_landed[v.r4], 16)

            def rsqrt(v):
                pool.wait_ge(e_mv, v.no + 1)
                reach(pool, e_shifted, v.no - 1)
                pool.sem_inc(passed["pool"], 1)
                nc.gpsimd.tensor_scalar(veps[v.r2][:], mv[v.r2][:, 1:2], EPS, None, ALU.add).then_inc(e_veps, 1)
                pool.wait_ge(e_veps, v.no + 1)
                nc.gpsimd.tensor_tensor(rstd[v.r2][:], veps[v.r2][:], minus_half[:], ALU.pow).then_inc(e_rstd, 1)

            def add_shift(v):
                if v.l in VECTOR_SHIFTS:
                    return
                pool.wait_ge(e_scaled, v.turns + 1)
                nc.gpsimd.tensor_tensor(y[v.r2][:], y[v.r2][:], shift[:, v.l, :], ALU.add).then_inc(e_shifted, 1)

            def out_rsqrt(v):
                if v.l < L - 1:
                    return
                n = v.no - ET * (L - 1)
                reach(pool, e_o, n - 1)
                pool.wait_ge(e_oveps, n + 1)
                nc.gpsimd.tensor_tensor(orstd[v.r2][:], oveps[v.r2][:], minus_half[:], ALU.pow).then_inc(e_orstd, 1)

            def scatter(v, ready, count):
                reach(pool, scattered[v.r4], 16 * v.use)
                pool.sem_inc(passed["pool"], 1)
                nc.gpsimd.tensor_copy(scatter_rows[v.r4][:], tile_rows(v, 2, 3)).then_inc(e_srows, 1)
                pool.wait_ge(e_srows, v.no + 1)
                pool.wait_ge(ready, count)
                pool.sem_inc(passed["pool"], 1)
                pool.indirect_dma_start(out if v.l == L - 1 else h_dram[v.l],
                                        bass.IndirectOffsetOnAxis(scatter_rows[v.r4][:, 0:1], 0), res[v.r4], None,
                                        bounds_check=N - 1, oob_is_err=False).then_inc(scattered[v.r4], 16)

            def scatter_h(v):
                if v.l < L - 1:
                    scatter(v, e_h, v.no + 1)

            def scatter_out(v):
                if v.l == L - 1:
                    scatter(v, e_o, v.no - ET * (L - 1) + 1)

            def slot(l, body, k):
                steps(l, body, k, (gather, 3), (gather_self, 2 if l in STORED_PRODUCT else 3), (gather_x, 1), (rsqrt, -1), (scatter_h, -3), (out_rsqrt, -3), (add_shift, -1),
                      (scatter_out, -5))

            all_tiles(pool, slot)
            for i in range(AB):
                pool.wait_ge(scattered[i], 16 * NB * L)

        def tile_rows(v, c0, c1):
            return rows_of[:, bass.ds(v.t, 1), c0:c1].rearrange("p a c -> p (a c)")

        def tensor_edges(pe):
            def turn(v):
                if v.l in STORED_PRODUCT:
                    return
                pe.wait_ge(self_landed[v.r4], 16 * (v.use + 1))
                reach(pe, e_low, v.turns - 1)
                for k in range(KC):
                    mm = pe.transpose(ps_t[v.r2][:, k * P:(k + 1) * P], self_in[v.r4][:, k * P:(k + 1) * P], ident[:])
                mm.then_inc(e_turned, 1)

            def sum_messages(v):
                pe.wait_ge(e_same, v.no + 1)
                pe.wait_ge(m_landed[v.r4], 16 * (v.use + 1))
                reach(pe, e_carry, v.no - 1)
                for k in range(KC):
                    mm = pe.matmul(ps_s[v.r2][:, k * P:(k + 1) * P], m_in[v.r4][:, k * P:(k + 1) * P], same[v.r2][:],
                                   start=True, stop=True)
                mm.then_inc(e_summed, 1)

            def product_self(v):
                reach(pe, e_z_sum, v.no - 1)
                if v.l in STORED_PRODUCT:
                    return
                pe.matmul(ps_z[v.r2][:], ones2[:], bias2[:, v.l, :], start=True, stop=False)
                pe.wait_ge(e_low, v.turns + 1)
                mm3(pe, ps_z[v.r2], hT_hi[v.r2], hT_lo[v.r2], v.l, False, True).then_inc(e_z_ready, 1)

            def product_mean(v):
                if v.l in WHOLE_PRODUCT:
                    pe.wait_ge(e_carry, v.no + 1)
                    for k in range(KC):
                        mm = pe.matmul(ps_a[v.r2][:], sumT[v.r2][:, k * P:(k + 1) * P], w_whole[:, k, :],
                                       start=k == 0, stop=k == KC - 1)
                    mm.then_inc(e_a_ready, 1)
                    return
                pe.wait_ge(e_slow, v.turns + 1)
                mm3(pe, ps_a[v.r2], sT_hi[v.r2], sT_lo[v.r2], L + v.l, True, True).then_inc(e_a_ready, 1)

            def slot(l, body, k):
                steps(l, body, k, (product_self, 0), (turn, 1), (sum_messages, 2), (product_mean, 0))

            all_tiles(pe, slot)

        def scalar_edges(act):
            def mean(v):
                if v.l in STORED_PRODUCT:
                    return
                act.wait_ge(e_a_ready, v.no + 1)
                reach(act, e_gained, v.no - 1)
                nc.scalar.activation(z_sb[v.r2], ps_a[v.r2][:], ACT.Identity,
                                     scale=rcount[:, bass.ds(v.t, 1)]).then_inc(e_mean, 1)

            def take_high(v):
                if v.l in STORED_PRODUCT:
                    return
                act.wait_ge(e_turned, v.turns + 1)
                reach(act, e_z_ready, v.turns - 1)
                nc.scalar.copy(flat(hT_hi[v.r2]), ps_t[v.r2][:]).then_inc(e_high, 1)

            def take_sum_high(v):
                if v.l in WHOLE_PRODUCT:
                    return
                act.wait_ge(e_carry, v.no + 1)
                reach(act, e_a_ready, v.no - 1)
                nc.scalar.copy(flat(sT_hi[v.r2]), sumT[v.r2]).then_inc(e_shigh, 1)

            def part(v):
                act.wait_ge(e_shifted, v.no + 1)
                reach(act, e_h, v.no - 1)
                nc.scalar.activation(neg[v.r2][:], y[v.r2][:], ACT.Relu, scale=-1.0).then_inc(e_parted, 1)

            def scale(v):
                if v.l in VECTOR_SHIFTS:
                    return
                act.wait_ge(e_gained, v.no + 1)
                act.wait_ge(e_rstd, v.no + 1)
                nc.scalar.activation(y[v.r2][:], y[v.r2][:], ACT.Identity, scale=rstd[v.r2][:, 0:1]).then_inc(e_scaled, 1)

            def take_over(v):
                if isinstance(v.t, int) and v.t == 0:
                    return
                act.wait_ge(e_same, v.no + 1)
                act.wait_ge(e_carry, v.no)
                for k in range(KC):
                    ins = nc.scalar.activation(over[v.r2][:, k * P:(k + 1) * P], carried[v.r2], ACT.Identity,
                                               scale=sumT[1 - v.r2][:, (k + 1) * P - 1:(k + 1) * P])
                ins.then_inc(e_taken_over, 1)

            def out_norm(v):
                if v.l < L - 1:
                    return
                act.wait_ge(e_orstd, v.no - ET * (L - 1) + 1)
                act.wait_ge(e_omean, v.no - ET * (L - 1) + 1)
                nc.scalar.activation(res[v.r4], res[v.r4], ACT.Identity, scale=orstd[v.r2][:, 0:1],
                                     bias=omean[v.r2][:, 0:1]).then_inc(e_o, 1)

            def slot(l, body, k):
                steps(l, body, k, (mean, -1), (take_sum_high, 1), (take_over, 2), (part, -2),
                      (take_high, 1), (scale, -1), (out_norm, -4))

            all_tiles(act, slot)

        def vector_edges(dve):
            def add_products(v):
                if v.l in STORED_PRODUCT:
                    dve.wait_ge(e_a_ready, v.no + 1)
                    dve.wait_ge(self_landed[v.r4], 16 * (v.use + 1))
                    nc.vector.scalar_tensor_tensor(z_sb[v.r2], ps_a[v.r2][:], rcount[:, bass.ds(v.t, 1)], self_in[v.r4],
                                                   ALU.mult, ALU.add).then_inc(e_z_sum, 1)
                    return
                dve.wait_ge(e_mean, v.turns + 1)
                nc.vector.tensor_tensor(z_sb[v.r2], z_sb[v.r2], ps_z[v.r2][:], ALU.add).then_inc(e_z_sum, 1)

            def take_low(v):
                if v.l in STORED_PRODUCT:
                    return
                dve.wait_ge(e_high, v.turns + 1)
                nc.vector.tensor_tensor(flat(hT_lo[v.r2]), ps_t[v.r2][:], flat(hT_hi[v.r2]).bitcast(F32),
                                        ALU.subtract).then_inc(e_low, 1)

            def carry(v):
                dve.wait_ge(e_summed, v.no + 1)
                if v.l in WHOLE_PRODUCT or (v.l == 1 and isinstance(v.t, int) and v.t < 2):
                    reach(dve, e_a_ready, v.no - 1)
                else:
                    reach(dve, e_slow, v.turns - 1)
                if isinstance(v.t, int) and v.t == 0:
                    nc.vector.tensor_copy(sumT[v.r2], ps_s[v.r2][:]).then_inc(e_carry, 1)
                    return
                dve.wait_ge(e_taken_over, v.no - v.l)
                nc.vector.tensor_tensor(sumT[v.r2], over[v.r2], ps_s[v.r2][:], ALU.add).then_inc(e_carry, 1)

            def take_sum_low(v):
                if v.l in WHOLE_PRODUCT:
                    return
                dve.wait_ge(e_shigh, v.turns + 1)
                nc.vector.tensor_tensor(flat(sT_lo[v.r2]), sumT[v.r2], flat(sT_hi[v.r2]).bitcast(F32),
                                        ALU.subtract).then_inc(e_slow, 1)

            def statistics(v):
                dve.wait_ge(e_z_sum, v.no + 1)
                nc.vector.bn_stats(stats[v.r2][:], z_sb[v.r2]).then_inc(e_stat, 1)

            def mean(v):
                dve.wait_ge(e_stat, v.no + 1)
                reach(dve, e_parted, v.no - 1)
                dve.sem_inc(passed["dve"], 1)
                nc.vector.bn_aggr(mv[v.r2][:], stats[v.r2][:]).then_inc(e_mv, 1)

            def normal(v):
                dve.wait_ge(e_mv, v.no + 1)
                nc.vector.scalar_tensor_tensor(y[v.r2][:], z_sb[v.r2], mv[v.r2][:, 0:1], gain[:, v.l, :],
                                               ALU.subtract, ALU.mult).then_inc(e_gained, 1)

            def scale_and_shift(v):
                if v.l not in VECTOR_SHIFTS:
                    return
                dve.wait_ge(e_gained, v.no + 1)
                dve.wait_ge(e_rstd, v.no + 1)
                nc.vector.scalar_tensor_tensor(y[v.r2][:], y[v.r2][:], rstd[v.r2][:, 0:1], shift[:, v.l, :],
                                               ALU.mult, ALU.add).then_inc(e_shifted, 1)

            def compare(v):
                reach(dve, e_summed, v.no - 1)
                reach(dve, e_carry, v.no - 1)
                here = dst_row[:, bass.ds(v.t * P + 1, P)]
                if not (isinstance(v.t, int) and v.t == 0):
                    nc.vector.tensor_scalar(carried[v.r2], here, dst_row[:, bass.ds(v.t * P, 1)], None, ALU.is_equal)
                nc.vector.tensor_scalar(same[v.r2][:], here, dst_col[:, bass.ds(v.t, 1)], None,
                                        ALU.is_equal).then_inc(e_same, 1)

            def prelu(v):
                dve.wait_ge(e_parted, v.no + 1)
                reach(dve, scattered[v.r4], 16 * v.use)
                nc.vector.scalar_tensor_tensor(res[v.r4], neg[v.r2][:], slope_less[:, 0:1], y[v.r2][:],
                                               ALU.mult, ALU.add).then_inc(e_h, 1)

            def out_sum(v):
                if v.l < L - 1:
                    return
                n = v.no - ET * (L - 1)
                dve.wait_ge(xe_landed[v.r4], 16 * (v.body + 1))
                dve.wait_ge(e_h, v.no + 1)
                nc.vector.tensor_tensor(res[v.r4], res[v.r4], xe_in[v.r4], ALU.add).then_inc(e_osum, 1)

            def out_statistics(v):
                if v.l < L - 1:
                    return
                n = v.no - ET * (L - 1)
                dve.wait_ge(e_osum, n + 1)
                nc.vector.bn_stats(ostats[v.r2][:], res[v.r4]).then_inc(e_ostat, 1)

            def out_mean(v):
                if v.l < L - 1:
                    return
                dve.wait_ge(e_ostat, v.no - ET * (L - 1) + 1)
                dve.sem_inc(passed["dve"], 1)
                nc.vector.bn_aggr(omv[v.r2][:], ostats[v.r2][:]).then_inc(e_omv, 1)

            def out_variance(v):
                if v.l < L - 1:
                    return
                dve.wait_ge(e_omv, v.no - ET * (L - 1) + 1)
                nc.vector.tensor_scalar(oveps[v.r2][:], omv[v.r2][:, 1:2], EPS, None, ALU.add).then_inc(e_oveps, 1)

            def out_shift(v):
                if v.l < L - 1:
                    return
                n = v.no - ET * (L - 1)
                dve.wait_ge(e_orstd, n + 1)
                reach(dve, e_o, n - 1)
                nc.vector.scalar_tensor_tensor(omean[v.r2][:], omv[v.r2][:, 0:1], -1.0, orstd[v.r2][:],
                                               ALU.mult, ALU.mult).then_inc(e_omean, 1)

            def slot(l, body, k):
                filled = ((compare, 3), (mean, -1)) if l in STORED_PRODUCT else ((mean, -1), (compare, 3))
                steps(l, body, k, (carry, 1), (add_products, -1), (out_statistics, -3), (statistics, -1),
                      (out_mean, -3), (out_variance, -3), *filled, (normal, -1), (take_sum_low, 1),
                      (scale_and_shift, -1), (prelu, -2), (take_low, 1), (out_shift, -3), (out_sum, -2))

            all_tiles(dve, slot)

        with nc.Block() as block:
            block.gpsimd(gpsimd_edges)
            block.tensor(tensor_edges)
            block.scalar(scalar_edges)
            block.vector(vector_edges)


def flat(t):
    return t[:].rearrange("p k n -> p (k n)")


def kernel(**inputs):
    import concourse.bacc as bacc
    from concourse.bass_utils import run_bass_kernel_spmd

    nc = bacc.Bacc("TRN2", target_bir_lowering=False, num_devices=1)
    arrays = {}

    def given(name, array):
        array = np.ascontiguousarray(array)
        arrays[f"in_{name}"] = array
        return nc.dram_tensor(f"in_{name}", array.shape, mybir.dt.from_np(array.dtype), kind="ExternalInput").ap()

    N = inputs["x"].shape[0]
    E = inputs["src"].shape[0]
    ET = -(-E // P)
    per_layer = lambda name: [given(f"{name}{l}", inputs[f"L0_gnn_{name}{l}"]) for l in range(L)]
    ident = given("ident", np.eye(P, dtype=np.float32))
    edge_no = given("edge_no", np.arange(ET * P, dtype=np.float32).reshape(ET, P))
    row_select = given("row_select", np.array([[0.0], [-1.0]], np.float32))
    dst_pad = given("dst_pad", np.array([-1] + [N] * (ET * P - E + 1), np.int32))
    src_pad = given("src_pad", np.zeros(P, np.int32))
    x = given("x", inputs["x"])
    out = nc.dram_tensor("out", x.shape, F32, kind="ExternalOutput").ap()
    build_program(nc, x, given("src", inputs["src"]), given("dst", inputs["dst"]),
                  per_layer("Wl"), per_layer("bl"), per_layer("Wr"), per_layer("g"), per_layer("b"),
                  given("a_prelu", inputs["L0_gnn_a_prelu"]), ident, edge_no, row_select, dst_pad, src_pad, out)
    result = run_bass_kernel_spmd(nc, [arrays], core_ids=[0])
    return result.results[0]["out"]
```
